# Optimizing a Trainium2 kernel written in Bass

```python
import numpy as np
import jax
import jax.numpy as jnp

def _softmax(x, axis=-1):
    return jax.nn.softmax(x, axis=axis)

def _gelu(x):
    return jax.nn.gelu(x, approximate=True)

def _silu(x):
    return jax.nn.silu(x)

def _sigmoid(x):
    return jax.nn.sigmoid(x)

def _layernorm(x, axis=-1, eps=1e-05):
    m = jnp.mean(x, axis=axis, keepdims=True)
    v = jnp.var(x, axis=axis, keepdims=True)
    return (x - m) / jnp.sqrt(v + eps)

def _scatter_add(tgt, idx, src, axis=0):
    return tgt.at[idx].add(src)

def _segment_sum(src, seg, n):
    return jax.ops.segment_sum(src, seg, n)
kernel_name = 'mk_seq_preln_d1_jaxref_r8_bc7deb'

def setup_inputs(seed: int=0):
    np.random.seed(seed)
    _w = jnp.asarray

    def _L0_attn_setup():
        import jax, jax.numpy as jnp
        import numpy as np
        B, S, D = (2, 512, 256)
        H, DK, DV = (16, 128, 128)
        SEG = 64
        UPDATE = 'delta'
        CAUSAL = True
        key = jax.random.key(seed)
        ks = jax.random.split(key, 6)
        s = 0.02
        return {'x': jax.random.normal(ks[0], (B, S, D), jnp.float32), 'Wq': jax.random.normal(ks[1], (D, H * DK), jnp.float32) * s, 'Wk': jax.random.normal(ks[2], (D, H * DK), jnp.float32) * s, 'Wv': jax.random.normal(ks[3], (D, H * DV), jnp.float32) * s, 'Wo': jax.random.normal(ks[4], (H * DV, D), jnp.float32) * s, 'betas': jax.random.normal(ks[5], (1, H, 1, DV), jnp.float32)}
    _L0_attn_in = _L0_attn_setup()

    def _L0_ffn_setup():
        import jax, jax.numpy as jnp
        import numpy as np
        E = 32
        K = 4
        G = 4
        TG = 2
        H = 256
        F = 128
        FS = 256
        SCALE = 2.0
        B, S = (2, 128)
        N = B * S
        CAP = 2 * (N * K // E)

        def _gate(x, gate_w, gate_bias):
            logits = x @ gate_w.T
            scores = jax.nn.sigmoid(logits)
            sc = scores + gate_bias
            n = x.shape[0]
            grp = sc.reshape(n, G, E // G)
            group_scores = jax.lax.top_k(grp, 2)[0].sum(-1)
            _, gidx = jax.lax.top_k(group_scores, TG)
            gmask = jnp.zeros((n, G), sc.dtype).at[jnp.arange(n)[:, None], gidx].set(1.0)
            smask = jnp.repeat(gmask, E // G, axis=1)
            tmp = jnp.where(smask > 0, sc, 0.0)
            _, topk_idx = jax.lax.top_k(tmp, K)
            topk_w = jnp.take_along_axis(scores, topk_idx, axis=1)
            topk_w = topk_w / (topk_w.sum(-1, keepdims=True) + 1e-20)
            return (topk_idx, topk_w * SCALE)

        def _moe(x, topk_idx, topk_w, w1, w2, w3):
            n = x.shape[0]
            flat_e = topk_idx.reshape(-1)
            oh = jax.nn.one_hot(flat_e, E, dtype=jnp.int32)
            pos = (jnp.cumsum(oh, axis=0) * oh).sum(-1) - 1
            keep = pos < CAP
            slot = jnp.where(keep, pos, CAP)
            x_rep = jnp.repeat(x, K, axis=0)
            buf = jnp.zeros((E, CAP, H), x.dtype).at[flat_e, slot].set(x_rep, mode='drop')
            h = jax.nn.silu(jnp.einsum('ech,ehf->ecf', buf, w1)) * jnp.einsum('ech,ehf->ecf', buf, w3)
            ob = jnp.einsum('ecf,efh->ech', h, w2)
            y = ob[flat_e, jnp.minimum(slot, CAP - 1)]
            y = jnp.where(keep[:, None], y, 0.0)
            return (y.reshape(n, K, H) * topk_w[:, :, None]).sum(1)
        key = jax.random.key(seed)
        ks = jax.random.split(key, 9)
        w = 0.02
        return {'hidden_states': jax.random.normal(ks[0], (B, S, H), jnp.float32), 'gate_w': jax.random.normal(ks[1], (E, H), jnp.float32) * w, 'gate_bias': jax.random.normal(ks[2], (E,), jnp.float32) * w, 'w1': jax.random.normal(ks[3], (E, H, F), jnp.float32) * w, 'w2': jax.random.normal(ks[4], (E, F, H), jnp.float32) * w, 'w3': jax.random.normal(ks[5], (E, H, F), jnp.float32) * w, 'shared_gate': jax.random.normal(ks[6], (H, FS), jnp.float32) * w, 'shared_up': jax.random.normal(ks[7], (H, FS), jnp.float32) * w, 'shared_down': jax.random.normal(ks[8], (FS, H), jnp.float32) * w}
    _L0_ffn_in = _L0_ffn_setup()
    _d = {'L0_attn_x': _L0_attn_in['x'], 'L0_attn_Wq': _L0_attn_in['Wq'], 'L0_attn_Wk': _L0_attn_in['Wk'], 'L0_attn_Wv': _L0_attn_in['Wv'], 'L0_attn_Wo': _L0_attn_in['Wo'], 'L0_attn_betas': _L0_attn_in['betas'], 'L0_ffn_gate_w': _L0_ffn_in['gate_w'], 'L0_ffn_gate_bias': _L0_ffn_in['gate_bias'], 'L0_ffn_w1': _L0_ffn_in['w1'], 'L0_ffn_w2': _L0_ffn_in['w2'], 'L0_ffn_w3': _L0_ffn_in['w3'], 'L0_ffn_shared_gate': _L0_ffn_in['shared_gate'], 'L0_ffn_shared_up': _L0_ffn_in['shared_up'], 'L0_ffn_shared_down': _L0_ffn_in['shared_down']}
    _x0 = _d['L0_attn_x']
    _d['L0_attn_x'] = jax.random.normal(jax.random.fold_in(jax.random.key(seed), 1), (2, 2048, 256), dtype=_x0.dtype)
    del _x0
    return _d

def reference(L0_attn_x, L0_attn_Wq, L0_attn_Wk, L0_attn_Wv, L0_attn_Wo, L0_attn_betas, L0_ffn_gate_w, L0_ffn_gate_bias, L0_ffn_w1, L0_ffn_w2, L0_ffn_w3, L0_ffn_shared_gate, L0_ffn_shared_up, L0_ffn_shared_down):

    def _L0_attn_ref(x, Wq, Wk, Wv, Wo, betas):
        import jax, jax.numpy as jnp
        import numpy as np
        B, S, D = (2, 512, 256)
        H, DK, DV = (16, 128, 128)
        SEG = 64
        UPDATE = 'delta'
        CAUSAL = True
        Bsz, seq, _ = x.shape
        nseg = seq // SEG
        q = (x @ Wq).reshape(Bsz, seq, H, DK).transpose(0, 2, 1, 3)
        k = (x @ Wk).reshape(Bsz, seq, H, DK).transpose(0, 2, 1, 3)
        v = (x @ Wv).reshape(Bsz, seq, H, DV).transpose(0, 2, 1, 3)
        qs = q.reshape(Bsz, H, nseg, SEG, DK).transpose(2, 0, 1, 3, 4)
        ks_ = k.reshape(Bsz, H, nseg, SEG, DK).transpose(2, 0, 1, 3, 4)
        vs = v.reshape(Bsz, H, nseg, SEG, DV).transpose(2, 0, 1, 3, 4)
        causal_mask = jnp.tril(jnp.ones((SEG, SEG), bool))
        scale = DK ** 0.5
        beta = jax.nn.sigmoid(betas)

        def step(carry, seg):
            mem, z = carry
            qq, kk, vv = seg
            sigma_q = jax.nn.elu(qq) + 1.0
            scores = jnp.einsum('bhsk,bhtk->bhst', qq, kk) / scale
            if CAUSAL:
                scores = jnp.where(causal_mask, scores, -jnp.inf)
            att_dot = jax.nn.softmax(scores, axis=-1) @ vv
            att_mem = sigma_q @ mem / (sigma_q @ z)
            sigma_k = jax.nn.elu(kk) + 1.0
            if UPDATE == 'linear':
                mem_new = mem + jnp.einsum('bhsk,bhsv->bhkv', sigma_k, vv)
            else:
                delta = vv - sigma_k @ mem / (sigma_k @ z)
                mem_new = mem + jnp.einsum('bhsk,bhsv->bhkv', sigma_k, delta)
            z_new = z + sigma_k.sum(axis=-2, keepdims=True).transpose(0, 1, 3, 2)
            att = beta * att_mem + (1.0 - beta) * att_dot
            out = att.reshape(Bsz, SEG, H * DV) @ Wo
            return ((mem_new, z_new), out)
        mem0 = jnp.zeros((Bsz, H, DK, DV), x.dtype)
        z0 = jnp.ones((Bsz, H, DK, 1), x.dtype) / DK
        _, outs = jax.lax.scan(step, (mem0, z0), (qs, ks_, vs))
        return outs.transpose(1, 0, 2, 3).reshape(Bsz, seq, D)

    def _L0_ffn_ref(hidden_states, gate_w, gate_bias, w1, w2, w3, shared_gate, shared_up, shared_down):
        import jax, jax.numpy as jnp
        import numpy as np
        E = 32
        K = 4
        G = 4
        TG = 2
        H = 256
        F = 128
        FS = 256
        SCALE = 2.0
        B, S = (2, 128)
        N = B * S
        CAP = 2 * (N * K // E)

        def _gate(x, gate_w, gate_bias):
            logits = x @ gate_w.T
            scores = jax.nn.sigmoid(logits)
            sc = scores + gate_bias
            n = x.shape[0]
            grp = sc.reshape(n, G, E // G)
            group_scores = jax.lax.top_k(grp, 2)[0].sum(-1)
            _, gidx = jax.lax.top_k(group_scores, TG)
            gmask = jnp.zeros((n, G), sc.dtype).at[jnp.arange(n)[:, None], gidx].set(1.0)
            smask = jnp.repeat(gmask, E // G, axis=1)
            tmp = jnp.where(smask > 0, sc, 0.0)
            _, topk_idx = jax.lax.top_k(tmp, K)
            topk_w = jnp.take_along_axis(scores, topk_idx, axis=1)
            topk_w = topk_w / (topk_w.sum(-1, keepdims=True) + 1e-20)
            return (topk_idx, topk_w * SCALE)

        def _moe(x, topk_idx, topk_w, w1, w2, w3):
            n = x.shape[0]
            flat_e = topk_idx.reshape(-1)
            oh = jax.nn.one_hot(flat_e, E, dtype=jnp.int32)
            pos = (jnp.cumsum(oh, axis=0) * oh).sum(-1) - 1
            keep = pos < CAP
            slot = jnp.where(keep, pos, CAP)
            x_rep = jnp.repeat(x, K, axis=0)
            buf = jnp.zeros((E, CAP, H), x.dtype).at[flat_e, slot].set(x_rep, mode='drop')
            h = jax.nn.silu(jnp.einsum('ech,ehf->ecf', buf, w1)) * jnp.einsum('ech,ehf->ecf', buf, w3)
            ob = jnp.einsum('ecf,efh->ech', h, w2)
            y = ob[flat_e, jnp.minimum(slot, CAP - 1)]
            y = jnp.where(keep[:, None], y, 0.0)
            return (y.reshape(n, K, H) * topk_w[:, :, None]).sum(1)
        b, s, h = hidden_states.shape
        x = hidden_states.reshape(-1, h)
        topk_idx, topk_w = _gate(x, gate_w, gate_bias)
        out = _moe(x, topk_idx, topk_w, w1, w2, w3)
        shared = jax.nn.silu(x @ shared_gate) * (x @ shared_up) @ shared_down
        return (out + shared).reshape(b, s, h)
    x = L0_attn_x
    x = x + _L0_attn_ref(_layernorm(x, axis=-1), L0_attn_Wq, L0_attn_Wk, L0_attn_Wv, L0_attn_Wo, L0_attn_betas)
    x = x + _L0_ffn_ref(_layernorm(x, axis=-1), L0_ffn_gate_w, L0_ffn_gate_bias, L0_ffn_w1, L0_ffn_w2, L0_ffn_w3, L0_ffn_shared_gate, L0_ffn_shared_up, L0_ffn_shared_down)
    return x

_drawn_inputs = setup_inputs


def setup_inputs(seed=0):
    import zlib

    import numpy as np

    out = dict(_drawn_inputs(seed))
    spreads = {}
    factors = {'L0_attn_Wq': 8.0,
     'L0_attn_Wk': 8.0,
     'L0_attn_betas': 3.295,
     'L0_ffn_gate_w': 8.0,
     'L0_ffn_gate_bias': 8.0,
     'L0_ffn_w1': 8.0,
     'L0_ffn_w2': 8.0,
     'L0_ffn_w3': 8.0,
     'L0_ffn_shared_gate': 3.413,
     'L0_ffn_shared_up': 3.386,
     'L0_ffn_shared_down': 3.375}
    for name, (base, spread) in spreads.items():
        noise = np.random.default_rng([zlib.crc32(name.encode()), seed]).standard_normal(out[name].shape)
        drawn = base * np.exp(spread * noise) if base else spread * noise
        out[name] = jnp.asarray(drawn.astype(out[name].dtype))
    for name, factor in factors.items():
        out[name] = (out[name] * factor).astype(out[name].dtype)
    return out
```

```python
import concourse.bass as bass
from concourse import mybir
from contextlib import ExitStack

fp32 = mybir.dt.float32
fp32r = mybir.dt.float32r
u32 = mybir.dt.uint32
i32 = mybir.dt.int32
ALU = mybir.AluOpType
ACT = mybir.ActivationFunctionType
AX = mybir.AxisListType

B, S, D = 2, 2048, 256
H, DK = 16, 128
SEG = 64
BLK = 2 * SEG
NBLK = S // BLK
NC = D // 128
HG = 2
NG = H // HG
T = HG * B
ZC = DK + 1
E, F, FS = 32, 128, 256
GR, GE = 4, 8
TOPK = 4
N = B * S
PIECES = H
QR = SEG // PIECES
CAP = 2 * (256 * TOPK // E)
ROW = D + E
QUART = N // 4
ZEROINGS = 64
SENT = -3.4028234663852886e38
BIG = 3.4028234663852886e38
LN_EPS = 1e-5
RSQRT_MAGIC = 1597463007.0
MASKED = -1e30
KSCALE = 1.0 / (DK ** 0.5)


def stand_alone(eng, noted):
    eng.sem_inc(noted, 1)


def link_on(eng, sem, base, noted=None):
    count = [0]

    def link(ins, alone=False):
        count[0] += 1
        ins.then_inc(sem, 1)
        eng.wait_ge(sem, base + count[0])
        if alone:
            stand_alone(eng, noted)
    return link


def attention(nc, ctx, io, scratch):
    def sb(name, shape, dt=fp32):
        return ctx.enter_context(nc.sbuf_tensor(name, shape, dt))

    def sem(name):
        return ctx.enter_context(nc.semaphore(name))

    w_hi = sb("w_hi", [128, NG, 3, NC, HG * DK], fp32r)
    w_lo = sb("w_lo", [128, NG, 3, NC, HG * DK], fp32r)
    w_in = sb("w_in", [128, 3, NC, HG * DK])
    wo = sb("wo", [128, H, D])
    mem = sb("mem", [128, H, B, ZC])
    x_in = sb("x_in", [128, B, D])
    x_res = sb("x_res", [128, B, D])
    gw, betas = x_res[0:E, 0, :], x_res[0:H, 1, 0:DK]
    xt_hi = sb("xt_hi", [128, NC, B, BLK], fp32r)
    xt_lo = sb("xt_lo", [128, NC, B, BLK], fp32r)
    sig = sb("sig", [128, 2, T, 4 * SEG])
    sigk = sb("sigk", [128, T, BLK])
    qraw = sb("qraw", [128, T, BLK])
    kraw = sb("kraw", [128, T, BLK])
    ex = sb("ex", [128, T, BLK])
    val_sb = sb("val_sb", [128, B, HG, DK])
    ksig = sb("ksig", [128, T, DK])
    sm = sb("sm", [128, T, SEG])
    smx = sb("smx", [128, T])
    ssum = sb("ssum", [128, T])
    sinv = sb("sinv", [128, T])
    pd = sb("pd", [128, T, BLK])
    pt = sb("pt", [128, T, BLK])
    cs = sb("cs", [128, T, BLK])
    am = sb("am", [128, 2, T, DK])
    att = sb("att", [128, B * PIECES, BLK])
    dl = [sb(f"dl{g}", [128, T, ZC]) for g in range(2)]
    rden = sb("rden", [128, HG, 2, B])
    mask = sb("mask", [128, SEG])
    ident = sb("ident", [128, 128])
    by_piece = sb("by_piece", [128, 128])
    by_piece_swapped = sb("by_piece_swapped", [128, 128])
    bt = sb("bt", [128, 4, H])
    beta, omb = bt[:, 2, :], bt[:, 3, :]
    st = sb("st", [128, B, 6])
    mv = sb("mv", [128, B, 2])
    rs = sb("rs", [128, B])
    nv = sb("nv", [128, 3, B])
    x1 = sb("x1", [128, B, D])
    xrow = sb("xrow", [128, B, ROW])
    x1t = sb("x1t", [128, NC, B, BLK])
    gwt = sb("gwt", [128, NC, E])
    gbias = sb("gbias", [128, B, E])
    eg = sb("eg", [128, B, E])
    score = sb("score", [128, B, E])
    scb = sb("scb", [128, B, E])
    g8 = sb("g8", [128, B, GR, 8])
    gsx = sb("gsx", [128, B, 10])
    gtop = sb("gtop", [128, B, 8])
    glist = sb("glist", [128, B, 8])
    grp = sb("grp", [128, B, 10])
    gm = sb("gm", [128, B, GR])
    tmpa = sb("tmpa", [128, B, E])
    tmpx = sb("tmpx", [128, B, E + 4])
    ttop = sb("ttop", [128, B, 8])
    tlist = sb("tlist", [128, B, 8])
    trp = sb("trp", [128, B, E + 4])
    pick = sb("pick", [128, B, E])
    wsel = sb("wsel", [128, B, E])
    wsum = sb("wsum", [128, 3, B])
    desc = sb("desc", [E, B, BLK])
    pickv = sb("pickv", [E, B, BLK])
    zero = sb("zero", [128, CAP * ROW // 128])

    def bank(name):
        return ctx.enter_context(nc.psum_tensor(name, [128, 512], fp32))
    chain = [bank("chain0"), bank("chain1")]
    bank_o = bank("bank_o")
    bank_q, bank_k, bank_v = bank("bank_q"), bank("bank_k"), bank("bank_v")
    bank_a, bank_s = bank("bank_a"), bank("bank_s")

    names = ("w_arrived w_hi_done w_lo_done wo_arrived bt_arrived bt_ready ident_ready "
             "gw_arrived gwt_mm gwt_ready gb_arrived const_ready zero_ready zeroed desc_ready "
             "x_arrived xres_arrived x_normed xt_mm xt_hi_ready xt_lo_ready "
             "q_mm k_mm v_mm s_mm kt_mm pt_mm ct_mm at_mm wo_mm "
             "q_raw q_exp q_min q_sig k_raw k_exp k_min k_sig k_placed v_ready ksig_ready "
             "s_masked s_max s_shifted s_exp s_sum s_inv p_half p_ready pt_ready cs_ready att_ready "
             "x1_ready x1_normed x1_stored x1t_mm x1t_ready x1t_stored lg_mm lg_exp "
             "row_stored pickt_mm pickv_ready pickv_stored ln1_step ln2_step gate_step "
             "bt_step dve_noted pool_noted").split()
    s = {n: sem(n) for n in names}
    num_mm = [sem(f"num_mm{j}") for j in range(HG)]
    upd_mm = [sem(f"upd_mm{j}") for j in range(HG)]
    den_inv = [sem(f"den_inv{j}") for j in range(HG)]
    dl_ready = [sem(f"dl_ready{j}") for j in range(HG)]
    am_ready = [sem(f"am_ready{j}") for j in range(HG)]
    mem_ready = [sem(f"mem_ready{j}") for j in range(HG)]

    SROWS = [slice(0, SEG), slice(SEG, BLK)]
    OTHER = [slice(SEG, BLK), slice(0, SEG)]
    GATE_STEPS, PICK_STEP, LN_STEPS = 20, 15, 14

    def blocks(eng, body):
        body(0, True, False)
        with eng.Fori(1, NBLK - 1) as blk:
            body(blk, False, False)
        body(NBLK - 1, False, True)

    block = ctx.enter_context(nc.Block())

    @block.sync
    def _(sp):
        def load_w(g):
            if g:
                sp.wait_ge(s["w_lo_done"], g)
            for m in range(3):
                w = io[("Wq", "Wk", "Wv")[m]].rearrange("(c p) n -> p c n", p=128)
                sp.dma_start(w_in[:, m, :, :], w[:, :, g * HG * DK:(g + 1) * HG * DK]
                             ).then_inc(s["w_arrived"], 16)

        x_blocks = io["x"].rearrange("b (n p) d -> n p b d", p=BLK)

        sp.dma_start(x_in[:, :, :], x_blocks[0]).then_inc(s["x_arrived"], 16)
        load_w(0)
        sp.dma_start(gw, io["gate_w"]).then_inc(s["gw_arrived"], 16)
        load_w(1)
        sp.dma_start(wo[:, :, :], io["Wo"].rearrange("(h p) n -> p h n", p=128)
                     ).then_inc(s["wo_arrived"], 16)
        sp.dma_start(gbias[:, :, :], io["gate_bias"].unsqueeze(0).unsqueeze(0)
                     .to_broadcast([128, B, E])).then_inc(s["gb_arrived"], 16)

        def body(blk, first, last):
            if first:
                for g in range(2, NG):
                    load_w(g)
            if not last:
                sp.wait_ge(s["xt_mm"], blk + 1)
                nxt = x_blocks[bass.ds(blk + 1, 1)] if not first else x_blocks[1:2]
                sp.dma_start(x_in[:, :, :], nxt.rearrange("n p b d -> p (n b) d")
                             ).then_inc(s["x_arrived"], 16)
            if not first:
                store_x1(blk)
            load_res(blk)
            if first:
                sp.wait_ge(s["zero_ready"], 1)
                y_flat = scratch["y_flat"]
                with sp.Fori(0, ZEROINGS) as a:
                    sp.dma_start(y_flat[bass.ds(a, 1), :, :].rearrange("a p n -> p (a n)"),
                                 zero[:, 0:y_flat.shape[2]]).then_inc(s["zeroed"], 16)
                sp.dma_start(scratch["rows"][N:N + CAP, :].rearrange("n d -> (n d)").rearrange(
                    "(p m) -> p m", p=128), zero[:, :]).then_inc(s["zeroed"], 16)
            else:
                store_rest(blk)

        def load_res(blk):
            if isinstance(blk, int) and blk == 0:
                sp.wait_ge(s["gwt_mm"], 1)
            cur = (x_blocks[blk:blk + 1] if isinstance(blk, int) else x_blocks[bass.ds(blk, 1)])
            cur = cur.rearrange("n p b d -> p (n b) d")
            sp.dma_start(x_res[:, :, :], cur).then_inc(s["xres_arrived"], 16)

        def at(ap, blk):
            return ap[blk - 1:blk] if isinstance(blk, int) else ap[bass.ds(blk - 1, 1)]

        def store_x1(blk):
            sp.wait_ge(s["x1_ready"], blk)
            sp.dma_start(at(scratch["x1"], blk).rearrange("n p d -> p (n d)"),
                         x1[:, :, :].rearrange("p b d -> p (b d)")).then_inc(s["x1_stored"], 16)

        def store_rest(blk):
            sp.wait_ge(s["x1t_ready"], blk)
            sp.dma_start(at(scratch["x1t"], blk).rearrange("n p d -> p (n d)"),
                         x1t[:, :, :, :].rearrange("p c b t -> p (c b t)")
                         ).then_inc(s["x1t_stored"], 16)
            sp.wait_ge(s["gate_step"], GATE_STEPS * blk)
            rows = scratch["rows"][0:N, :].rearrange("(b n p) d -> n p b d", b=B, p=BLK)
            rows = at(rows, blk).rearrange("n p b d -> p (n b) d")
            sp.dma_start(rows, xrow[:, :, :]).then_inc(s["row_stored"], 16)
            sp.wait_ge(s["pickv_ready"], blk)
            picks = scratch["picks"].rearrange("e (b n t) -> n e b t", b=B, t=BLK)
            sp.dma_start(at(picks, blk).rearrange("n e b t -> e (n b) t"), pickv[:, :, :]
                         ).then_inc(s["pickv_stored"], 16)

        blocks(sp, body)
        store_x1(NBLK)
        store_rest(NBLK)
        sp.wait_ge(s["zeroed"], 16 * (ZEROINGS + 1))
        sp.wait_ge(s["x1_stored"], 16 * NBLK)
        sp.wait_ge(s["x1t_stored"], 16 * NBLK)
        sp.wait_ge(s["row_stored"], 16 * NBLK)
        sp.wait_ge(s["pickv_stored"], 16 * NBLK)

    @block.gpsimd
    def _(pool):
        nc.gpsimd.memset(ident[:, :], 0.0).then_inc(s["ident_ready"], 1)
        pool.wait_ge(s["ident_ready"], 1)
        nc.gpsimd.affine_select(out=ident[:, :], in_=ident[:, :], compare_op=ALU.not_equal,
                                fill=1.0, base=0, pattern=[[-1, 128]], channel_multiplier=1
                                ).then_inc(s["ident_ready"], 1)
        nc.gpsimd.memset(by_piece[:, :], 0.0).then_inc(s["ident_ready"], 1)
        nc.gpsimd.memset(by_piece_swapped[:, :], 0.0).then_inc(s["ident_ready"], 1)
        pool.wait_ge(s["ident_ready"], 4)
        for m, base, seg_step in ((by_piece, 0, -SEG), (by_piece_swapped, -SEG, SEG)):
            nc.gpsimd.affine_select(out=m[:, :], in_=m[:, :],
                                    compare_op=ALU.not_equal, fill=1.0, base=base,
                                    pattern=[[-1, PIECES], [seg_step, 2], [-PIECES, QR]],
                                    channel_multiplier=1).then_inc(s["ident_ready"], 1)
        pool.wait_ge(s["ident_ready"], 6)
        nc.gpsimd.memset(mask[:, :], 0.0).then_inc(s["const_ready"], 1)
        pool.wait_ge(s["const_ready"], 1)
        for half in range(2):
            rows = slice(SEG * half, SEG * half + SEG)
            nc.gpsimd.affine_select(out=mask[rows, :], in_=mask[rows, :], compare_op=ALU.is_ge,
                                    fill=MASKED, base=0, pattern=[[-1, SEG]],
                                    channel_multiplier=1).then_inc(s["const_ready"], 1)
            pool.wait_ge(s["const_ready"], 2 + half)
        nc.gpsimd.memset(pd[:, :, :], 0.0).then_inc(s["const_ready"], 1)
        nc.gpsimd.iota(desc[:, :, :], pattern=[[-S, B], [-1, BLK]], base=N, channel_multiplier=0,
                       allow_small_or_imprecise_dtypes=True).then_inc(s["desc_ready"], 1)
        pool.wait_ge(s["const_ready"], 4)

        def step(n, first=False):
            pool.wait_ge(s["s_max"], n + 1)
            nc.gpsimd.tensor_tensor(sm[:, :, :], sm[:, :, :],
                                    smx[:, :].unsqueeze(2).to_broadcast([128, T, SEG]),
                                    ALU.subtract).then_inc(s["s_shifted"], 1)
            pool.wait_ge(s["s_inv"], n + 1)
            if not first:
                pool.wait_ge(s["pt_mm"], n)
            for seg in range(2):
                r = SROWS[seg]
                if seg:
                    pool.wait_ge(s["p_half"], n + 1)
                ins = nc.gpsimd.tensor_tensor(pd[r, :, r], sm[r, :, :],
                                              sinv[r, :].unsqueeze(2).to_broadcast([SEG, T, SEG]),
                                              ALU.mult
                                              ).then_inc(s[("p_half", "p_ready")[seg]], 1)
            pool.wait_ge(s["p_ready"], n + 1)

        def place_keys(n, par, first=False):
            pool.wait_ge(s["k_sig"], n + 1)
            if not first:
                pool.wait_ge(num_mm[HG - 1], 2 * n - 2)
            stand_alone(pool, s["pool_noted"])
            for seg in range(2):
                ins = nc.gpsimd.tensor_copy(sig[:, par, :, 3 * SEG * seg:3 * SEG * seg + SEG],
                                            sigk[:, :, SROWS[seg]])
            ins.then_inc(s["k_placed"], 1)

        place_keys(0, 0, True)
        step(0, True)
        place_keys(1, 1, True)
        step(1)
        with pool.Fori(1, NBLK * NG // 2) as m:
            place_keys(2 * m, 0)
            step(2 * m)
            place_keys(2 * m + 1, 1)
            step(2 * m + 1)

    @block.scalar
    def _(act):
        act.dma_start(betas, io["betas"].rearrange("a h b d -> (a h b) d")
                      ).then_inc(s["bt_arrived"], 16)

        def split_hi(g):
            act.wait_ge(s["w_arrived"], 48 * (g + 1))
            nc.scalar.activation(w_hi[:, g, :, :, :], w_in[:, :, :, :], ACT.Copy
                                 ).then_inc(s["w_hi_done"], 1)

        def xt_hi_part(count):
            act.wait_ge(s["xt_mm"], count)
            nc.scalar.activation(xt_hi[:, :, :, :].rearrange("p c b t -> p (c b t)"), bank_a[:, :],
                                 ACT.Copy).then_inc(s["xt_hi_ready"], 1)

        def queries(n, first_ever=False):
            act.wait_ge(s["q_mm"], n + 1)
            if not first_ever:
                act.wait_ge(s["s_mm"], n)
            nc.scalar.activation(qraw[:, :, :], bank_q[:, :], ACT.Copy).then_inc(s["q_raw"], 1)
            if not first_ever:
                act.wait_ge(s["k_sig"], n)
            nc.scalar.activation(ex[:, :, :], bank_q[:, :], ACT.Exp).then_inc(s["q_exp"], 1)

        def keys(n):
            act.wait_ge(s["k_mm"], n + 1)
            nc.scalar.activation(kraw[:, :, :], bank_k[:, :], ACT.Copy).then_inc(s["k_raw"], 1)
            act.wait_ge(s["q_sig"], n + 1)
            nc.scalar.activation(ex[:, :, :], bank_k[:, :], ACT.Exp).then_inc(s["k_exp"], 1)

        def values(n):
            act.wait_ge(s["v_mm"], n + 1)
            nc.scalar.activation(val_sb[:, :, :, :], bank_v[:, :], ACT.Copy
                                 ).then_inc(s["v_ready"], 1)

        def key_rows(n):
            act.wait_ge(s["kt_mm"], n + 1)
            nc.scalar.activation(ksig[:, :, :], bank_k[:, :], ACT.Copy
                                 ).then_inc(s["ksig_ready"], 1)

        def read_out(n, g, seg):
            for j in range(HG):
                act.wait_ge(den_inv[j], 2 * n + seg + 1)
                r = OTHER[seg]
                for b in range(B):
                    ins = nc.scalar.activation(am[r, g % 2, j * B + b, :],
                                               chain[j][r, b * ZC:b * ZC + DK], ACT.Copy,
                                               scale=rden[r, j, seg, b:b + 1])
                ins.then_inc(am_ready[j], 1)

        split_hi(0)
        xt_hi_part(1)
        act.wait_ge(s["gwt_mm"], 1)
        nc.scalar.activation(bt[:, 1, :], bank_s[:, NC * E:NC * E + H], ACT.Exp, scale=-1.0
                             ).then_inc(s["bt_step"], 1)
        nc.scalar.activation(gwt[:, :, :], bank_s[:, 0:NC * E], ACT.Copy).then_inc(s["gwt_ready"], 1)
        split_hi(1)
        queries(0, True)
        keys(0)
        values(0)
        key_rows(0)
        act.wait_ge(s["bt_ready"], 1)

        def body(blk, first, last):
            for g in range(NG):
                n = blk * NG + g
                nxt = not (last and g == NG - 1)
                if not (first and g < 2):
                    act.wait_ge(s["at_mm"], n - 1)
                read_out(n, g, 0)
                act.wait_ge(s["s_shifted"], n + 1)
                nc.scalar.activation(sm[:, :, :], sm[:, :, :], ACT.Exp, scale=KSCALE
                                     ).then_inc(s["s_exp"], 1)
                if nxt:
                    queries(n + 1)
                act.wait_ge(s["pt_mm"], n + 1)
                nc.scalar.activation(pt[:, :, :], bank_v[:, :], ACT.Copy).then_inc(s["pt_ready"], 1)
                if g == 3 and not first:
                    act.wait_ge(s["lg_mm"], blk)
                    nc.scalar.activation(eg[:, :, :], bank_a[:, 0:B * E], ACT.Exp, scale=-1.0
                                         ).then_inc(s["lg_exp"], 1)
                if g == 2 and not first:
                    side_x1t(blk)
                read_out(n, g, 1)
                if nxt:
                    keys(n + 1)
                act.wait_ge(s["ct_mm"], n + 1)
                if not (first and g == 0):
                    act.wait_ge(s["att_ready"], 2 * n)
                for j in range(HG):
                    nc.scalar.activation(cs[:, j * B:j * B + B, :],
                                         bank_q[:, j * B * BLK:(j + 1) * B * BLK], ACT.Copy,
                                         scale=omb[:, HG * g + j:HG * g + j + 1]
                                         ).then_inc(s["cs_ready"], 1)
                if first and g + 2 < NG:
                    split_hi(g + 2)
                if nxt:
                    values(n + 1)
                if g == NG - 1 and not first:
                    act.wait_ge(s["x1t_stored"], 16 * blk)
                if g == NG - 2 and not last:
                    act.wait_ge(s["v_mm"], n + 2)
                    xt_hi_part(blk + 2)
                if nxt:
                    key_rows(n + 1)

        def side_x1t(blk):
            act.wait_ge(s["x1t_mm"], blk)
            nc.scalar.activation(x1t[:, :, :, :].rearrange("p c b t -> p (c b t)"), bank_a[:, :],
                                 ACT.Copy).then_inc(s["x1t_ready"], 1)

        blocks(act, body)
        side_x1t(NBLK)
        act.wait_ge(s["lg_mm"], NBLK)
        nc.scalar.activation(eg[:, :, :], bank_a[:, 0:B * E], ACT.Exp, scale=-1.0
                             ).then_inc(s["lg_exp"], 1)

    @block.vector
    def _(dve):
        def split_lo(g):
            dve.wait_ge(s["w_hi_done"], g + 1)
            nc.vector.tensor_tensor(w_lo[:, g, :, :, :].rearrange("p m c n -> p (m c n)"),
                                    w_in[:, :, :, :].rearrange("p m c n -> p (m c n)"),
                                    w_hi[:, g, :, :, :].rearrange("p m c n -> p (m c n)")
                                    .bitcast(fp32), ALU.subtract).then_inc(s["w_lo_done"], 1)

        def layernorm(link, out, x_t):
            for b in range(B):
                ins = nc.vector.bn_stats(out=st[:, b, :], in_=x_t[:, b, :])
            link(ins, alone=True)
            for b in range(B):
                ins = nc.vector.bn_aggr(out=mv[:, b, :], in_=st[:, b, :])
            link(ins)
            link(nc.vector.tensor_scalar_add(nv[:, 0, :], mv[:, :, 1], LN_EPS))
            link(nc.vector.tensor_single_scalar(nv[:, 1, :].bitcast(i32), nv[:, 0, :].bitcast(i32),
                                                1, ALU.logical_shift_right))
            link(nc.vector.tensor_scalar(rs[:, :].bitcast(i32), nv[:, 1, :].bitcast(i32), -1.0,
                                         RSQRT_MAGIC, ALU.mult, ALU.add))
            for _ in range(3):
                link(nc.vector.tensor_tensor(nv[:, 1, :], rs[:, :], rs[:, :], ALU.mult))
                link(nc.vector.scalar_tensor_tensor(out=nv[:, 2, :], in0=nv[:, 1, :], scalar=-0.5,
                                                    in1=nv[:, 0, :], op0=ALU.mult, op1=ALU.mult))
                link(nc.vector.scalar_tensor_tensor(out=rs[:, :], in0=nv[:, 2, :], scalar=1.5,
                                                    in1=rs[:, :], op0=ALU.add, op1=ALU.mult))
            for b in range(B):
                ins = nc.vector.tensor_scalar(out[:, b, 0:D], x_t[:, b, :], mv[:, b, 0:1],
                                              rs[:, b:b + 1], ALU.subtract, ALU.mult)
            return ins

        def norm_x(count):
            dve.wait_ge(s["x_arrived"], 16 * count)
            link = link_on(dve, s["ln1_step"], (count - 1) * LN_STEPS, s["dve_noted"])
            layernorm(link, x_in, x_in).then_inc(s["x_normed"], 1)

        def xt_lo_part(count):
            dve.wait_ge(s["xt_hi_ready"], count)
            nc.vector.tensor_tensor(xt_lo[:, :, :, :].rearrange("p c b t -> p (c b t)"),
                                    bank_a[:, :],
                                    xt_hi[:, :, :, :].rearrange("p c b t -> p (c b t)")
                                    .bitcast(fp32), ALU.subtract).then_inc(s["xt_lo_ready"], 1)

        def sigma_q(n, par):
            dve.wait_ge(s["q_exp"], n + 1)
            nc.vector.tensor_scalar_min(ex[:, :, :], ex[:, :, :], 1.0).then_inc(s["q_min"], 1)
            dve.wait_ge(s["q_min"], n + 1)
            nc.vector.scalar_tensor_tensor(
                out=sig[:, par, :, SEG:3 * SEG],
                in0=bank_q[:, :].rearrange("p (t c) -> p t c", t=T), scalar=1.0,
                in1=ex[:, :, :], op0=ALU.add, op1=ALU.max).then_inc(s["q_sig"], 1)

        def sigma_k(n):
            dve.wait_ge(s["k_exp"], n + 1)
            nc.vector.tensor_scalar_min(ex[:, :, :], ex[:, :, :], 1.0).then_inc(s["k_min"], 1)
            dve.wait_ge(s["k_min"], n + 1)
            if not (isinstance(n, int) and n == 0):
                dve.wait_ge(s["k_placed"], n)
                dve.wait_ge(s["kt_mm"], n)
            nc.vector.scalar_tensor_tensor(
                out=sigk[:, :, :], in0=bank_k[:, :].rearrange("p (t c) -> p t c", t=T),
                scalar=1.0, in1=ex[:, :, :], op0=ALU.add, op1=ALU.max).then_inc(s["k_sig"], 1)

        def delta(n, seg):
            if seg == 0:
                dve.wait_ge(s["v_ready"], n + 1)
            for j in range(HG):
                dve.wait_ge(num_mm[j], 2 * n + seg + 1)
                nc.vector.reciprocal(rden[:, j, seg, :],
                                     chain[j][:, DK:DK + ZC + 1:ZC]).then_inc(den_inv[j], 1)
                dve.wait_ge(den_inv[j], 2 * n + seg + 1)
                r = SROWS[seg]
                for b in range(B):
                    ins = nc.vector.scalar_tensor_tensor(
                        out=dl[seg][r, j * B + b, 0:DK], in0=chain[j][r, b * ZC:b * ZC + DK],
                        scalar=rden[r, j, seg, b:b + 1], in1=val_sb[r, b, j, :],
                        op0=ALU.mult, op1=ALU.subtract)
                ins.then_inc(dl_ready[j], 1)

        def state(n, g, seg):
            for j in range(HG):
                dve.wait_ge(upd_mm[j], 2 * n + seg + 1)
                m = mem[:, HG * g + j, :, :].rearrange("p b z -> p (b z)")
                nc.vector.tensor_tensor(m, m, chain[j][:, 0:B * ZC], ALU.subtract
                                        ).then_inc(mem_ready[j], 1)

        def attend(n, g, blk):
            dve.wait_ge(s["at_mm"], n + 1)
            dve.wait_ge(s["cs_ready"], 2 * n + 2)
            if g == 0 and not (isinstance(n, int) and n == 0):
                dve.wait_ge(s["wo_mm"], blk)
            for j in range(HG):
                h = HG * g + j
                read = bank_a[:, j * B * BLK:(j + 1) * B * BLK].rearrange(
                    "p (a s q) -> p a s q", s=2, q=QR)
                soft = cs[:, j * B:j * B + B, :].rearrange("p b (a s q) -> p (b a) s q", s=2, q=QR)
                for seg in range(2):
                    c = seg * SEG + h * QR
                    ins = nc.vector.scalar_tensor_tensor(
                        out=att[:, :, c:c + QR], in0=read[:, :, seg, :], scalar=beta[:, h:h + 1],
                        in1=soft[:, :, seg, :], op0=ALU.mult, op1=ALU.add)
                ins.then_inc(s["att_ready"], 1)

        def residual(blk):
            dve.wait_ge(s["wo_mm"], blk)
            dve.wait_ge(s["xres_arrived"], 16 * blk)
            nc.vector.tensor_tensor(x1[:, :, :].rearrange("p b d -> p (b d)"), bank_o[:, :],
                                    x_res[:, :, :].rearrange("p b d -> p (b d)"), ALU.add
                                    ).then_inc(s["x1_ready"], 1)
            dve.wait_ge(s["x1_ready"], blk)
            link = link_on(dve, s["ln2_step"], (blk - 1) * LN_STEPS, s["dve_noted"])
            layernorm(link, xrow, x1).then_inc(s["x1_normed"], 1)

        def gate(blk):
            dve.wait_ge(s["lg_exp"], blk)
            link = link_on(dve, s["gate_step"], (blk - 1) * GATE_STEPS, s["dve_noted"])
            v = nc.vector
            link(v.tensor_scalar_add(eg[:, :, :], eg[:, :, :], 1.0))
            link(v.reciprocal(score[:, :, :], eg[:, :, :]))
            link(v.tensor_tensor(scb[:, :, :], score[:, :, :], gbias[:, :, :], ALU.add), True)
            for b in range(B):
                for i in range(GR):
                    ins = v.max(g8[:, b, i, :], scb[:, b, GE * i:GE * i + GE])
            link(ins)
            link(v.tensor_tensor(gsx[:, :, 0:GR], g8[:, :, :, 0], g8[:, :, :, 1], ALU.add), True)
            for b in range(B):
                ins = v.max(gtop[:, b, :], gsx[:, b, :])
            link(ins)
            link(v.tensor_copy(glist[:, :, 0:2], gtop[:, :, 0:2]), True)
            for b in range(B):
                ins = v.match_replace(out=grp[:, b, :], in_to_replace=glist[:, b, :],
                                      in_values=gsx[:, b, :], imm_value=BIG)
            link(ins)
            link(v.tensor_scalar(gm[:, :, :], grp[:, :, 0:GR], BIG, None, ALU.is_equal))
            link(v.tensor_tensor(tmpa[:, :, :].rearrange("p b (g e) -> p b g e", g=GR),
                                 scb[:, :, :].rearrange("p b (g e) -> p b g e", g=GR),
                                 gm[:, :, :].unsqueeze(3).to_broadcast([128, B, GR, GE]), ALU.mult))
            link(v.tensor_scalar_add(tmpx[:, :, 0:E], tmpa[:, :, :], 0.0), True)
            for b in range(B):
                ins = v.max(ttop[:, b, :], tmpx[:, b, 0:E])
            link(ins)
            link(v.tensor_copy(tlist[:, :, 0:TOPK], ttop[:, :, 0:TOPK]), True)
            for b in range(B):
                ins = v.match_replace(out=trp[:, b, :], in_to_replace=tlist[:, b, :],
                                      in_values=tmpx[:, b, :], imm_value=BIG)
            link(ins)
            link(v.tensor_scalar(pick[:, :, :], trp[:, :, 0:E], BIG, None, ALU.is_equal))
            link(v.tensor_tensor(wsel[:, :, :], score[:, :, :], pick[:, :, :], ALU.mult))
            link(v.tensor_reduce(wsum[:, 0, :], wsel[:, :, :], axis=AX.X, op=ALU.add))
            link(v.tensor_scalar_add(wsum[:, 1, :], wsum[:, 0, :], 1e-20))
            link(v.reciprocal(wsum[:, 2, :], wsum[:, 1, :]))
            for b in range(B):
                ins = v.tensor_scalar(xrow[:, b, D:ROW], wsel[:, b, :], wsum[:, 2, b:b + 1], 2.0,
                                      ALU.mult, ALU.mult)
            link(ins)

        def picks(blk):
            dve.wait_ge(s["pickt_mm"], blk)
            dve.wait_ge(s["desc_ready"], blk)
            pk = bank_a[0:E, 0:B * BLK].rearrange("p (b t) -> p b t", b=B)
            nc.vector.tensor_tensor(pickv[:, :, :], pk, desc[:, :, :], ALU.mult
                                    ).then_inc(s["pickv_ready"], 1)
            dve.wait_ge(s["pickv_ready"], blk)
            nc.vector.tensor_scalar_add(desc[:, :, :], desc[:, :, :], -float(BLK)
                                        ).then_inc(s["desc_ready"], 1)

        nc.vector.memset(mem[:, :, :, 0:DK], 0.0)
        nc.vector.memset(mem[:, :, :, DK:ZC], 1.0 / DK)
        for seg in range(2):
            nc.vector.memset(dl[seg][OTHER[seg], :, :], 0.0)
            nc.vector.memset(dl[seg][SROWS[seg], :, DK:ZC], -1.0)
        nc.vector.memset(gsx[:, :, :], SENT)
        nc.vector.memset(glist[:, :, :], SENT)
        nc.vector.memset(tmpx[:, :, :], SENT)
        nc.vector.memset(tlist[:, :, :], SENT)
        nc.vector.memset(zero[:, :], 0.0).then_inc(s["zero_ready"], 1)
        dve.wait_ge(s["zero_ready"], 1)
        norm_x(1)
        split_lo(0)
        xt_lo_part(1)
        dve.wait_ge(s["bt_step"], 1)
        link = link_on(dve, s["bt_step"], 1)
        link(nc.vector.tensor_scalar_add(bt[:, 0, :], bt[:, 1, :], 1.0))
        link(nc.vector.reciprocal(beta, bt[:, 0, :]))
        nc.vector.tensor_scalar(omb, beta, -1.0, 1.0, ALU.mult, ALU.add).then_inc(s["bt_ready"], 1)
        split_lo(1)
        sigma_q(0, 0)
        sigma_k(0)
        dve.wait_ge(s["const_ready"], 4)
        dve.wait_ge(s["gb_arrived"], 16)

        def body(blk, first, last):
            for g in range(NG):
                n = blk * NG + g
                nxt = not (last and g == NG - 1)
                dve.wait_ge(s["s_mm"], n + 1)
                for seg in range(2):
                    r = SROWS[seg]
                    ins = nc.vector.tensor_tensor(
                        sm[r, :, :], bank_s[:, :].rearrange("p (t c) -> p t c", t=T)[r, :, r],
                        mask[r, :].unsqueeze(1).to_broadcast([SEG, T, SEG]), ALU.add)
                ins.then_inc(s["s_masked"], 1)
                dve.wait_ge(s["s_masked"], n + 1)
                nc.vector.tensor_reduce(smx[:, :], sm[:, :, :], axis=AX.X, op=ALU.max
                                        ).then_inc(s["s_max"], 1)
                delta(n, 0)
                if not (first and g == 0):
                    attend(n - 1, (g - 1) % NG, blk)
                dve.wait_ge(s["s_exp"], n + 1)
                nc.vector.tensor_reduce(ssum[:, :], sm[:, :, :], axis=AX.X, op=ALU.add
                                        ).then_inc(s["s_sum"], 1)
                dve.wait_ge(s["s_sum"], n + 1)
                nc.vector.reciprocal(sinv[:, :], ssum[:, :]).then_inc(s["s_inv"], 1)
                state(n, g, 0)
                if nxt:
                    sigma_q(n + 1, (g + 1) % 2)
                delta(n, 1)
                if nxt:
                    sigma_k(n + 1)
                state(n, g, 1)
                if first and g + 2 < NG:
                    split_lo(g + 2)
                if g == 0 and not first:
                    residual(blk)
                if g == 3 and not first:
                    gate(blk)
                if g == 5 and not first:
                    picks(blk)
                if g == 4 and not last:
                    norm_x(blk + 2)
                if g == NG - 1 and not first:
                    dve.wait_ge(s["x1_stored"], 16 * blk)
                    dve.wait_ge(s["row_stored"], 16 * blk)
                    dve.wait_ge(s["pickv_stored"], 16 * blk)
                if g == NG - 2 and not last:
                    dve.wait_ge(s["v_mm"], n + 2)
                    xt_lo_part(blk + 2)

        blocks(dve, body)
        attend(NBLK * NG - 1, NG - 1, None)
        residual(NBLK)
        gate(NBLK)
        picks(NBLK)

    @block.tensor
    def _(pe):
        mm = nc.tensor.matmul

        def x_transposes():
            for c in range(NC):
                for b in range(B):
                    ins = nc.tensor.transpose(bank_a[:, (c * B + b) * BLK:(c * B + b + 1) * BLK],
                                              x_in[:, b, c * 128:(c + 1) * 128], ident[:, :])
            ins.then_inc(s["xt_mm"], 1)

        def project_t(out_bank, g, m):
            for j in range(HG):
                out = out_bank[:, j * B * BLK:(j + 1) * B * BLK]
                col = slice(j * DK, (j + 1) * DK)
                parts = [(w, x, c) for w, x in ((w_hi, xt_hi), (w_hi, xt_lo), (w_lo, xt_hi))
                         for c in range(NC)]
                for i, (w, x, c) in enumerate(parts):
                    ins = mm(out, w[:, g, m, c, col], x[:, c, :, :].rearrange("p b t -> p (b t)"),
                             start=i == 0, stop=i == len(parts) - 1)
            return ins

        def project_v(g):
            for b in range(B):
                out = bank_v[:, b * HG * DK:(b + 1) * HG * DK]
                parts = [(w, x, c) for w, x in ((w_hi, xt_hi), (w_hi, xt_lo), (w_lo, xt_hi))
                         for c in range(NC)]
                for i, (w, x, c) in enumerate(parts):
                    ins = mm(out, x[:, c, b, :], w[:, g, 2, c, :],
                             start=i == 0, stop=i == len(parts) - 1)
            return ins

        def scores(n, first_ever):
            pe.wait_ge(s["k_raw"], n + 1)
            pe.wait_ge(s["q_raw"], n + 1)
            if not first_ever:
                pe.wait_ge(s["s_masked"], n)
            for t in range(T):
                ins = mm(bank_s[:, t * BLK:(t + 1) * BLK],
                         qraw[:, t, :], kraw[:, t, :], start=True, stop=True)
            ins.then_inc(s["s_mm"], 1)

        def key_transposes(n):
            pe.wait_ge(s["k_sig"], n + 1)
            for t in range(T):
                ins = nc.tensor.transpose(bank_k[:, t * DK:(t + 1) * DK], sigk[:, t, :],
                                          ident[:, :])
            ins.then_inc(s["kt_mm"], 1)

        def numerators(n, g, seg):
            for j in range(HG):
                if not (isinstance(n, int) and n == 0 and seg == 0):
                    pe.wait_ge(mem_ready[j], 2 * n + seg)
                for b in range(B):
                    ins = mm(chain[j][:, b * ZC:(b + 1) * ZC],
                             sig[:, g % 2, j * B + b, seg * BLK:(seg + 1) * BLK],
                             mem[:, HG * g + j, b, :], start=True, stop=True)
                ins.then_inc(num_mm[j], 1)

        def updates(n, seg):
            for j in range(HG):
                pe.wait_ge(dl_ready[j], 2 * n + seg + 1)
                pe.wait_ge(am_ready[j], 2 * n + seg + 1)
                for b in range(B):
                    ins = mm(chain[j][:, b * ZC:(b + 1) * ZC], ksig[:, j * B + b, :],
                             dl[seg][:, j * B + b, :], start=True, stop=True)
                ins.then_inc(upd_mm[j], 1)

        def read_transposes(n, par):
            pe.wait_ge(am_ready[0], 2 * n + 2)
            pe.wait_ge(am_ready[1], 2 * n + 2)
            for t in range(T):
                ins = nc.tensor.transpose(bank_a[:, t * BLK:(t + 1) * BLK], am[:, par, t, :],
                                          by_piece_swapped[:, :])
            ins.then_inc(s["at_mm"], 1)

        def project_out(lo, hi, n=None):
            if lo == 0:
                pe.wait_ge(s["att_ready"], 2 * n)
            for i in range(lo, hi):
                for b in range(B):
                    ins = mm(bank_o[:, b * D:(b + 1) * D], att[:, b * PIECES + i, :], wo[:, i, :],
                             start=(i == 0 and b == 0), stop=(i == PIECES - 1),
                             skip_group_check=True)
            if hi == PIECES:
                ins.then_inc(s["wo_mm"], 1)

        def x1_transposes(blk):
            pe.wait_ge(s["x1_normed"], blk)
            for c in range(NC):
                for b in range(B):
                    ins = nc.tensor.transpose(bank_a[:, (c * B + b) * BLK:(c * B + b + 1) * BLK],
                                              xrow[:, b, c * 128:(c + 1) * 128], ident[:, :])
            ins.then_inc(s["x1t_mm"], 1)

        def logits(blk):
            pe.wait_ge(s["x1t_ready"], blk)
            for b in range(B):
                for c in range(NC):
                    ins = mm(bank_a[:, b * E:(b + 1) * E], x1t[:, c, b, :], gwt[:, c, :],
                             start=c == 0, stop=c == NC - 1)
            ins.then_inc(s["lg_mm"], 1)

        def pick_transposes(blk):
            pe.wait_ge(s["gate_step"], GATE_STEPS * (blk - 1) + PICK_STEP)
            for b in range(B):
                ins = nc.tensor.transpose(bank_a[0:E, b * BLK:(b + 1) * BLK], pick[:, b, :],
                                          ident[:, :])
            ins.then_inc(s["pickt_mm"], 1)

        pe.wait_ge(s["ident_ready"], 6)
        pe.wait_ge(s["x_normed"], 1)
        x_transposes()
        pe.wait_ge(s["gw_arrived"], 16)
        for c in range(NC):
            ins = nc.tensor.transpose(bank_s[:, c * E:(c + 1) * E], gw[:, c * 128:(c + 1) * 128],
                                      ident[0:E, 0:E])
        pe.wait_ge(s["bt_arrived"], 16)
        nc.tensor.transpose(bank_s[:, NC * E:NC * E + H], betas, ident[0:H, 0:H]
                            ).then_inc(s["gwt_mm"], 1)
        pe.wait_ge(s["xt_lo_ready"], 1)
        pe.wait_ge(s["w_lo_done"], 1)
        project_t(bank_q, 0, 0).then_inc(s["q_mm"], 1)
        project_t(bank_k, 0, 1).then_inc(s["k_mm"], 1)
        project_v(0).then_inc(s["v_mm"], 1)
        pe.wait_ge(s["gwt_ready"], 1)
        scores(0, True)
        key_transposes(0)
        pe.wait_ge(s["wo_arrived"], 16)

        def body(blk, first, last):
            for g in range(NG):
                n = blk * NG + g
                gn = (g + 1) % NG
                nxt = not (last and g == NG - 1)
                pe.wait_ge(s["q_sig"], n + 1)
                pe.wait_ge(s["k_placed"], n + 1)
                numerators(n, g, 0)
                if not (first and g == 0):
                    if not first and g == 3:
                        pe.wait_ge(s["x1t_ready"], blk)
                    if not first and g == 4:
                        pe.wait_ge(s["lg_exp"], blk)
                    if not first and g == 6:
                        pe.wait_ge(s["pickv_ready"], blk)
                    if not last and g == NG - 1:
                        pe.wait_ge(s["xt_lo_ready"], blk + 2)
                    read_transposes(n - 1, (g - 1) % 2)
                if nxt:
                    if first and g + 1 < NG:
                        pe.wait_ge(s["w_lo_done"], g + 2)
                    if not (first and g == 0):
                        pe.wait_ge(s["cs_ready"], 2 * n)
                    project_t(bank_q, gn, 0).then_inc(s["q_mm"], 1)
                pe.wait_ge(s["ksig_ready"], n + 1)
                updates(n, 0)
                if g == 0 and not first:
                    project_out(0, 6, n)
                elif not first or g:
                    pe.wait_ge(s["att_ready"], 2 * n)
                if g == 2 and not first:
                    x1_transposes(blk)
                if g == 3 and not first:
                    logits(blk)
                if g == 5 and not first:
                    pick_transposes(blk)
                if g == NG - 2 and not last:
                    pe.wait_ge(s["x_normed"], blk + 2)
                    x_transposes()
                pe.wait_ge(s["p_ready"], n + 1)
                pe.wait_ge(s["v_ready"], n + 1)
                for t in range(T):
                    ins = nc.tensor.transpose(bank_v[:, t * BLK:(t + 1) * BLK], pd[:, t, :],
                                              by_piece[:, :])
                ins.then_inc(s["pt_mm"], 1)
                numerators(n, g, 1)
                if g == 0 and not first:
                    project_out(6, 11)
                if nxt:
                    project_t(bank_k, gn, 1).then_inc(s["k_mm"], 1)
                pe.wait_ge(s["pt_ready"], n + 1)
                if nxt:
                    pe.wait_ge(s["q_sig"], n + 2)
                else:
                    pe.wait_ge(s["cs_ready"], 2 * n)
                for t in range(T):
                    ins = mm(bank_q[:, t * BLK:(t + 1) * BLK], val_sb[:, t % B, t // B, :],
                             pt[:, t, :], start=True, stop=True)
                ins.then_inc(s["ct_mm"], 1)
                updates(n, 1)
                if g == 0 and not first:
                    project_out(11, PIECES)
                if nxt:
                    project_v(gn).then_inc(s["v_mm"], 1)
                    scores(n + 1, False)
                    key_transposes(n + 1)

        blocks(pe, body)
        read_transposes(NBLK * NG - 1, (NG - 1) % 2)
        project_out(0, PIECES, NBLK * NG)
        x1_transposes(NBLK)
        logits(NBLK)
        pick_transposes(NBLK)


def experts(nc, ctx, io, scratch, out):
    def sb(name, shape, dt=fp32):
        return ctx.enter_context(nc.sbuf_tensor(name, shape, dt))

    def sem(name):
        return ctx.enter_context(nc.semaphore(name))

    EB = 4
    NB = E // EB
    TG = 2
    NTG = NBLK // TG
    AHEAD = 2
    FC = FS // 128
    QUARTERS = N // QUART
    YB = 4

    xt = sb("xt_all", [128, NBLK, NC, B, BLK])
    acc = sb("acc", [128, NBLK, B, D])
    w13 = sb("w13", [128, E, NC, 2, F])
    w2 = sb("w2_all", [128, E, D])
    sg = sb("sg", [128, NC, FS])
    su = sb("su", [128, NC, FS])
    sd = sb("sd", [128, FC, D])
    id2 = sb("id2", [64, 64])
    vq = sb("vq", [128, QUART])
    cand = sb("cand", [128, CAP])
    cm = sb("cm", [E, QUARTERS, CAP])
    sel = sb("sel", [E, CAP])
    spare = sb("spare", [E, CAP])
    idxf = sb("idxf", [E, 3, CAP])
    idx = sb("idx", [CAP, E], u32)
    ic = sb("ic", [CAP, 2, EB], u32)
    rows = sb("rows_in", [CAP, 2, EB, ROW])
    wc = sb("wc", [CAP, 2, EB])
    rt = sb("rt", [128, EB, NC, CAP])
    hs = sb("hs", [CAP, EB, F])
    hh = sb("hh", [CAP, EB, F])
    ht = sb("ht", [128, EB, CAP])
    ys = sb("ys", [CAP, 2, EB, D])
    sil = sb("sil", [128, FC, TG * B * BLK])
    sh = sb("sh", [128, FC, TG * B * BLK])

    def bank(name):
        return ctx.enter_context(nc.psum_tensor(name, [128, 512], fp32))
    bank_g = [bank("bank_g0"), bank("bank_g1")]
    bank_u = [bank("bank_u0"), bank("bank_u1")]
    bank_d = bank("bank_d")
    bank_t = bank("bank_t")
    bank_h = [bank("bank_h0"), bank("bank_h1")]

    names = ("vq_arrived cm_arrived xt_arrived acc_arrived shared_arrived id_ready spare_ready "
             "top_step sel_mm idx_ready g_mm u_mm sil_ready sh_ready d_mm acc_ready "
             "idx_copied added t_mm rt_ready h_mm silu_ready hh_ready ht_mm ht_ready y_mm ys_ready "
             "wc_ready out_ready out_stored pool_noted pe_noted").split()
    s = {n: sem("p2_" + n) for n in names}
    we_arrived = [sem(f"we_arrived{i}") for i in range(2)]
    gathered = [sem(f"gathered{i}") for i in range(2)]
    y_sems = [sem(f"y_arrived{k}") for k in range(NBLK // YB)]
    ROUNDS = CAP // 8

    def batches(eng, batch):
        for i in range(2):
            batch(i, i, i + AHEAD)
        with eng.Fori(1, (NTG - AHEAD) // 2) as pair:
            for par in range(2):
                batch(2 * pair + par, par, 2 * pair + par + AHEAD)
        for i in range(NTG - AHEAD, NB):
            batch(i, i % 2, None)

    def span(ap, i, n):
        return ap[i * n:(i + 1) * n] if isinstance(i, int) else ap[bass.ds(i * n, n)]

    block = ctx.enter_context(nc.Block())

    @block.sync
    def _(sp):
        for q in range(QUARTERS):
            sp.dma_start(vq[q * E:(q + 1) * E, :], scratch["picks"][:, q * QUART:(q + 1) * QUART]
                         ).then_inc(s["vq_arrived"], 16)
        for t, n in ((sg, "shared_gate"), (su, "shared_up"), (sd, "shared_down")):
            sp.dma_start(t[:, :, :], io[n].rearrange("(c p) f -> p c f", p=128)
                         ).then_inc(s["shared_arrived"], 16)
        sp.dma_start(xt[:, :, :, :, :].rearrange("p n c b t -> p n (c b t)"),
                     scratch["x1t"].rearrange("n p d -> p n d")).then_inc(s["xt_arrived"], 16)
        sp.dma_start(acc[:, :, :, :].rearrange("p n b d -> p n (b d)"),
                     scratch["x1"].rearrange("n p d -> p n d")).then_inc(s["acc_arrived"], 16)

        def load_batch(i, par):
            e = slice(i * EB, (i + 1) * EB) if isinstance(i, int) else bass.ds(i * EB, EB)
            for which, n in enumerate(("w1", "w3")):
                sp.dma_start(w13[:, e, :, which, :].rearrange("p e c f -> p (e c) f"),
                             io[n][e].rearrange("e (c p) f -> p (e c) f", p=128)
                             ).then_inc(we_arrived[par], 16)
            sp.dma_start(w2[:, e, :], io["w2"][e].rearrange("e p d -> p e d")
                         ).then_inc(we_arrived[par], 16)

        load_batch(0, 0)
        load_batch(1, 1)
        sp.wait_ge(s["top_step"], 2 * ROUNDS)
        for q in range(QUARTERS):
            sp.dma_start(cm[:, q, :], cand[q * E:(q + 1) * E, :]).then_inc(s["cm_arrived"], 16)
        with sp.Fori(1, NB // 2) as pair:
            for par in range(2):
                sp.wait_ge(we_arrived[par], 48 * pair)
                load_batch(2 * pair + par, par)
        sp.wait_ge(s["added"], 16 * E)
        sp.wait_ge(s["d_mm"], TG * NTG)
        y = scratch["y"][0:N, :].rearrange("(b n p) d -> p n b d", b=B, p=BLK)
        yt = xt[:, :, :, :, :].rearrange("p n c b t -> p n (c b t)").rearrange(
            "p n (b d) -> p n b d", b=B)
        o = out.rearrange("b (n p) d -> p n b d", p=BLK)
        for k in range(NBLK // YB):
            for b in range(B):
                sp.dma_start(yt[:, k * YB:(k + 1) * YB, b, :], y[:, k * YB:(k + 1) * YB, b, :]
                             ).then_inc(y_sems[k], 16)
        for k in range(NBLK // YB):
            sp.wait_ge(s["out_ready"], k + 1)
            for b in range(B):
                sp.dma_start(o[:, k * YB:(k + 1) * YB, b, :], acc[:, k * YB:(k + 1) * YB, b, :]
                             ).then_inc(s["out_stored"], 16)
        sp.wait_ge(s["out_stored"], 16 * B * (NBLK // YB))

    @block.gpsimd
    def _(pool):
        nc.gpsimd.memset(id2[:, :], 0.0).then_inc(s["id_ready"], 1)
        pool.wait_ge(s["id_ready"], 1)
        nc.gpsimd.affine_select(out=id2[:, :], in_=id2[:, :], compare_op=ALU.not_equal,
                                fill=1.0, base=0, pattern=[[-1, 64]], channel_multiplier=1
                                ).then_inc(s["id_ready"], 1)
        nc.gpsimd.iota(spare[:, :], pattern=[[1, CAP]], base=0, channel_multiplier=0,
                       allow_small_or_imprecise_dtypes=True).then_inc(s["spare_ready"], 1)
        pool.wait_ge(s["idx_ready"], 1)

        def gather(i, par, wait=True):
            if wait:
                pool.wait_ge(s["added"], 16 * EB * (i - 1))
                pool.wait_ge(s["wc_ready"], i - 1)
                pool.wait_ge(s["t_mm"], i - 1)
                stand_alone(pool, s["pool_noted"])
            src = idx[:, i * EB:(i + 1) * EB] if isinstance(i, int) else idx[:, bass.ds(i * EB, EB)]
            nc.gpsimd.tensor_copy(ic[:, par, :], src).then_inc(s["idx_copied"], 1)
            pool.wait_ge(s["idx_copied"], i + 1)
            stand_alone(pool, s["pool_noted"])
            for k in range(EB):
                pool.indirect_dma_start(
                    out=rows[:, par, k, :], out_offset=None, in_=scratch["rows"],
                    in_offset=bass.IndirectOffsetOnAxis(ap=ic[:, par, k:k + 1], axis=0),
                    bounds_check=N + CAP - 1).then_inc(gathered[par], 16)

        def scatter(i, par):
            pool.wait_ge(s["ys_ready"], i + 1)
            for k in range(EB):
                if not (isinstance(i, int) and i == 0 and k == 0):
                    pool.wait_ge(s["added"], 16 * (EB * i + k))
                    stand_alone(pool, s["pool_noted"])
                pool.indirect_dma_start(
                    out=scratch["y"],
                    out_offset=bass.IndirectOffsetOnAxis(ap=ic[:, par, k:k + 1], axis=0),
                    in_=ys[:, par, k, :], in_offset=None, bounds_check=N + CAP - 1,
                    compute_op=ALU.add).then_inc(s["added"], 16)

        gather(0, 0, False)
        gather(1, 1, False)
        scatter(0, 0)
        with pool.Fori(0, NB // 2 - 1) as pair:
            for par in range(2):
                gather(2 * pair + par + 2, par)
                scatter(2 * pair + par + 1, 1 - par)
        scatter(NB - 1, (NB - 1) % 2)
        pool.wait_ge(s["added"], 16 * E)

    @block.scalar
    def _(act):
        def shared_silu(g):
            for fc in range(FC):
                act.wait_ge(s["g_mm"], FC * g + fc + 1)
                if not (isinstance(g, int) and g == 0):
                    act.wait_ge(s["sh_ready"], FC * (g - 1) + fc + 1)
                nc.scalar.activation(sil[:, fc, :], bank_g[fc][:, :], ACT.Silu
                                     ).then_inc(s["sil_ready"], 1)

        for g in range(AHEAD):
            shared_silu(g)

        def batch(i, par, group):
            act.wait_ge(s["t_mm"], i + 1)
            nc.scalar.activation(rt[:, :, :, :], bank_t[:, :], ACT.Copy).then_inc(s["rt_ready"], 1)
            if group is not None:
                act_shared = lambda: shared_silu(group)
                act_shared()
            act.wait_ge(s["h_mm"], i + 1)
            for half in range(2):
                h = bank_h[half][0:CAP, :].rearrange("p (k w f) -> p k w f", k=2, w=2)
                ins = nc.scalar.activation(hs[:, 2 * half:2 * half + 2, :], h[:, :, 0, :], ACT.Silu)
            ins.then_inc(s["silu_ready"], 1)

        batches(act, batch)

    @block.vector
    def _(dve):
        def shared_mul(g):
            for fc in range(FC):
                dve.wait_ge(s["sil_ready"], FC * g + fc + 1)
                dve.wait_ge(s["u_mm"], FC * g + fc + 1)
                if not (isinstance(g, int) and g == 0):
                    dve.wait_ge(s["d_mm"], TG * g)
                nc.vector.tensor_tensor(sh[:, fc, :], sil[:, fc, :], bank_u[fc][:, :], ALU.mult
                                        ).then_inc(s["sh_ready"], 1)

        def shared_add(g):
            for k in range(TG):
                dve.wait_ge(s["d_mm"], TG * g + k + 1)
                a = (acc[:, TG * g + k, :, :].rearrange("p b d -> p (b d)") if isinstance(g, int)
                     else acc[:, bass.ds(TG * g + k, 1), :, :].rearrange("p n b d -> p (n b d)"))
                nc.vector.tensor_tensor(a, a, bank_d[:, :], ALU.add).then_inc(s["acc_ready"], 1)

        link = link_on(dve, s["top_step"], 0)

        def top8(out, values, r):
            link(nc.vector.max(out[:, 8 * r:8 * r + 8], values))
            link(nc.vector.match_replace(out=values, in_to_replace=out[:, 8 * r:8 * r + 8],
                                         in_values=values, imm_value=-1.0))

        dve.wait_ge(s["vq_arrived"], 16 * QUARTERS)
        for r in range(ROUNDS):
            top8(cand, vq[:, :], r)
            if r == ROUNDS // 2 - 1:
                shared_mul(0)
            if r == ROUNDS - 2:
                dve.wait_ge(s["acc_arrived"], 16)
                shared_add(0)
        shared_mul(1)
        dve.wait_ge(s["cm_arrived"], 16 * QUARTERS)
        for r in range(ROUNDS):
            top8(sel, cm[:, :, :].rearrange("p q c -> p (q c)"), r)
        dve.wait_ge(s["spare_ready"], 1)
        link(nc.vector.scalar_tensor_tensor(out=idxf[:, 0, :], in0=sel[:, :], scalar=0.0,
                                            in1=spare[:, :], op0=ALU.is_equal, op1=ALU.mult))
        link(nc.vector.scalar_tensor_tensor(out=idxf[:, 1, :], in0=sel[:, :], scalar=-1.0,
                                            in1=idxf[:, 0, :], op0=ALU.mult, op1=ALU.add))
        link(nc.vector.tensor_scalar_add(idxf[:, 2, :], idxf[:, 1, :], float(N)))
        shared_add(1)
        dve.wait_ge(s["sel_mm"], 1)
        nc.vector.tensor_copy(idx[:, :], bank_t[0:CAP, 0:E]).then_inc(s["idx_ready"], 1)

        def batch(i, par, group):
            if isinstance(i, int):
                dve.wait_ge(gathered[par], 16 * EB * (i // 2 + 1))
            else:
                dve.wait_ge(gathered[par], 8 * EB * (i - par) + 16 * EB)
            for k in range(EB):
                e = i * EB + k
                col = (rows[:, par, k, D + e:D + e + 1] if isinstance(i, int)
                       else rows[:, par, k, bass.ds(D + e, 1)])
                ins = nc.vector.tensor_copy(wc[:, par, k:k + 1], col)
            ins.then_inc(s["wc_ready"], 1)
            if group is not None:
                shared_mul(group)
            dve.wait_ge(s["silu_ready"], i + 1)
            for half in range(2):
                h = bank_h[half][0:CAP, :].rearrange("p (k w f) -> p k w f", k=2, w=2)
                ins = nc.vector.tensor_tensor(hh[:, 2 * half:2 * half + 2, :],
                                              hs[:, 2 * half:2 * half + 2, :], h[:, :, 1, :],
                                              ALU.mult)
            ins.then_inc(s["hh_ready"], 1)
            if group is not None:
                shared_add(group)
            dve.wait_ge(s["ht_mm"], i + 1)
            nc.vector.tensor_copy(ht[:, :, :], bank_t[:, 0:EB * CAP]).then_inc(s["ht_ready"], 1)
            dve.wait_ge(s["y_mm"], i + 1)
            for k in range(EB):
                ins = nc.vector.tensor_scalar(
                    ys[:, par, k, :], bank_h[k // 2][0:CAP, (k % 2) * D:(k % 2 + 1) * D],
                    wc[:, par, k:k + 1], None, ALU.mult)
            ins.then_inc(s["ys_ready"], 1)

        batches(dve, batch)
        for k in range(NBLK // YB):
            dve.wait_ge(y_sems[k], 16 * B)
            a = acc[:, k * YB:(k + 1) * YB, :, :].rearrange("p n b d -> p (n b d)")
            y = xt[:, k * YB:(k + 1) * YB, :, :, :].rearrange("p n c b t -> p (n c b t)")
            nc.vector.tensor_tensor(a, a, y, ALU.add).then_inc(s["out_ready"], 1)

    @block.tensor
    def _(pe):
        mm = nc.tensor.matmul

        def shared_up(g, fc):
            x = (xt[:, TG * g:TG * g + TG] if isinstance(g, int) else xt[:, bass.ds(TG * g, TG)])
            if not (isinstance(g, int) and g == 0):
                pe.wait_ge(s["sh_ready"], FC * (g - 1) + fc + 1)
            for w, bank_w, done in ((sg, bank_g, "g_mm"), (su, bank_u, "u_mm")):
                for c in range(NC):
                    ins = mm(bank_w[fc][:, :], w[:, c, fc * 128:(fc + 1) * 128],
                             x[:, :, c, :, :].rearrange("p n b t -> p n (b t)"),
                             start=c == 0, stop=c == NC - 1)
                ins.then_inc(s[done], 1)

        def shared_down(g):
            pe.wait_ge(s["sh_ready"], FC * g + FC)
            for k in range(TG):
                if k or not (isinstance(g, int) and g == 0):
                    pe.wait_ge(s["acc_ready"], TG * g + k)
                for b in range(B):
                    for fc in range(FC):
                        col = (k * B + b) * BLK
                        ins = mm(bank_d[:, b * D:(b + 1) * D], sh[:, fc, col:col + BLK],
                                 sd[:, fc, :], start=fc == 0, stop=fc == FC - 1)
                ins.then_inc(s["d_mm"], 1)

        pe.wait_ge(s["shared_arrived"], 48)
        pe.wait_ge(s["xt_arrived"], 16)
        for g in range(AHEAD):
            for fc in range(FC):
                shared_up(g, fc)
            shared_down(g)
        pe.wait_ge(s["id_ready"], 2)
        pe.wait_ge(s["top_step"], 4 * ROUNDS + 3)
        nc.tensor.transpose(bank_t[0:CAP, 0:E], idxf[:, 2, :], id2[0:E, 0:E]
                            ).then_inc(s["sel_mm"], 1)
        pe.wait_ge(s["idx_ready"], 1)

        def batch(i, par, group):
            if isinstance(i, int):
                pe.wait_ge(gathered[par], 16 * EB * (i // 2 + 1))
                pe.wait_ge(we_arrived[par], 48 * (i // 2 + 1))
            else:
                pe.wait_ge(gathered[par], 8 * EB * (i - par) + 16 * EB)
                pe.wait_ge(we_arrived[par], 24 * (i - par) + 48)
            if isinstance(i, int) and i == 0:
                pass
            else:
                pe.wait_ge(s["ht_ready"], i)
            stand_alone(pe, s["pe_noted"])
            for k in range(EB):
                for c in range(NC):
                    ins = nc.tensor.transpose(
                        bank_t[:, (k * NC + c) * CAP:(k * NC + c + 1) * CAP],
                        rows[:, par, k, c * 128:(c + 1) * 128], id2[:, :])
            ins.then_inc(s["t_mm"], 1)
            if group is not None:
                shared_up(group, 0)
            pe.wait_ge(s["rt_ready"], i + 1)
            if not (isinstance(i, int) and i == 0):
                pe.wait_ge(s["ys_ready"], i)
            for k in range(EB):
                for c in range(NC):
                    e = i * EB + k
                    w = (w13[:, e:e + 1, c, :, :] if isinstance(i, int)
                         else w13[:, bass.ds(e, 1), c, :, :])
                    ins = mm(bank_h[k // 2][0:CAP, (k % 2) * 2 * F:(k % 2 + 1) * 2 * F],
                             rt[:, k, c, :], w.rearrange("p e w f -> p (e w f)"),
                             start=c == 0, stop=c == NC - 1)
            ins.then_inc(s["h_mm"], 1)
            if group is not None:
                shared_up(group, 1)
            pe.wait_ge(s["hh_ready"], i + 1)
            stand_alone(pe, s["pe_noted"])
            for k in range(EB):
                ins = nc.tensor.transpose(bank_t[:, k * CAP:(k + 1) * CAP], hh[:, k, :], id2[:, :])
            ins.then_inc(s["ht_mm"], 1)
            if group is not None:
                shared_down(group)
            pe.wait_ge(s["ht_ready"], i + 1)
            for k in range(EB):
                e = i * EB + k
                w = w2[:, e:e + 1, :] if isinstance(i, int) else w2[:, bass.ds(e, 1), :]
                ins = mm(bank_h[k // 2][0:CAP, (k % 2) * D:(k % 2 + 1) * D], ht[:, k, :],
                         w.rearrange("p e d -> p (e d)"), start=True, stop=True)
            ins.then_inc(s["y_mm"], 1)

        batches(pe, batch)


def build(nc, args, out):
    io = dict(zip(("x", "Wq", "Wk", "Wv", "Wo", "betas", "gate_w", "gate_bias", "w1", "w2", "w3",
                   "shared_gate", "shared_up", "shared_down"), args))
    scratch = {
        "x1": nc.dram_tensor("x1_rows", (NBLK, 128, B * D), fp32).ap(),
        "x1t": nc.dram_tensor("x1_normed_t", (NBLK, 128, NC * B * BLK), fp32).ap(),
        "rows": nc.dram_tensor("expert_rows", (N + CAP, ROW), fp32).ap(),
        "picks": nc.dram_tensor("picks", (E, N), fp32).ap(),
        "y": nc.dram_tensor("expert_sums", (N + CAP, D), fp32).ap(),
    }
    scratch["y_flat"] = scratch["y"].rearrange("n d -> (n d)").rearrange(
        "(a p m) -> a p m", a=ZEROINGS, p=128)
    with ExitStack() as ctx:
        attention(nc, ctx, io, scratch)
    with ExitStack() as ctx:
        experts(nc, ctx, io, scratch, out)


_INS = ['L0_attn_x', 'L0_attn_Wq', 'L0_attn_Wk', 'L0_attn_Wv', 'L0_attn_Wo', 'L0_attn_betas',
        'L0_ffn_gate_w', 'L0_ffn_gate_bias', 'L0_ffn_w1', 'L0_ffn_w2', 'L0_ffn_w3',
        'L0_ffn_shared_gate', 'L0_ffn_shared_up', 'L0_ffn_shared_down']
_OUTS = [((2, 2048, 256), 'float32')]


def kernel(**inputs):
    import numpy as _np
    import concourse.bacc as _bacc
    from concourse import mybir as _mybir
    from concourse.bass_utils import run_bass_kernel_spmd as _run

    nc = _bacc.Bacc("TRN2", target_bir_lowering=False, num_devices=1)
    arrays, args = {}, []
    for name in _INS:
        a = _np.ascontiguousarray(inputs[name])
        arrays[f"in_{name}_dram"] = a
        args.append(nc.dram_tensor(f"in_{name}_dram", a.shape, _mybir.dt.from_np(a.dtype),
                                   kind="ExternalInput").ap())
    outs = []
    for i, (shape, dtype) in enumerate(_OUTS):
        dt = _mybir.dt.from_np(_np.dtype(dtype))
        outs.append(nc.dram_tensor(f"out_{i}_dram", shape, dt, kind="ExternalOutput").ap())
    build(nc, args, outs[0])
    r = _run(nc, [arrays], core_ids=[0])
    got = tuple(r.results[0][f"out_{i}_dram"] for i in range(len(_OUTS)))
    return got[0]
```

```python
import concourse.bass as bass
from concourse import mybir
from contextlib import ExitStack

fp32 = mybir.dt.float32
fp32r = mybir.dt.float32r
u32 = mybir.dt.uint32
i32 = mybir.dt.int32
ALU = mybir.AluOpType
ACT = mybir.ActivationFunctionType
AX = mybir.AxisListType

B, S, D = 2, 2048, 256
H, DK = 16, 128
SEG = 64
BLK = 2 * SEG
NBLK = S // BLK
NC = D // 128
HG = 2
NG = H // HG
T = HG * B
ZC = DK + 1
E, F, FS = 32, 128, 256
GR, GE = 4, 8
TOPK = 4
N = B * S
PIECES = H
QR = SEG // PIECES
CAP = 2 * (256 * TOPK // E)
ROW = D + E
QUART = N // 4
YPART = (N + CAP) * D // NBLK // 128
ZEROS = YPART // 5
SENT = -3.4028234663852886e38
BIG = 3.4028234663852886e38
LN_EPS = 1e-5
RSQRT_MAGIC = 1597463007.0
MASKED = -1e30
KSCALE = 1.0 / (DK ** 0.5)


def stand_alone(eng, noted):
    eng.sem_inc(noted, 1)


def link_on(eng, sem, base, noted=None):
    count = [0]

    def link(ins, alone=False):
        count[0] += 1
        ins.then_inc(sem, 1)
        eng.wait_ge(sem, base + count[0])
        if alone:
            stand_alone(eng, noted)
    return link


def attention(nc, ctx, io, scratch):
    def sb(name, shape, dt=fp32):
        return ctx.enter_context(nc.sbuf_tensor(name, shape, dt))

    def sem(name):
        return ctx.enter_context(nc.semaphore(name))

    w_hi = sb("w_hi", [128, NG, 3, NC, HG * DK], fp32r)
    w_lo = sb("w_lo", [128, NG, 3, NC, HG * DK], fp32r)
    w_in = sb("w_in", [128, 3, NC, HG * DK])
    wo = sb("wo", [128, H, D])
    mem = sb("mem", [128, H, B, ZC])
    x_in = sb("x_in", [128, B, D])
    x_res = sb("x_res", [128, B, D])
    gw, betas = x_res[0:E, 0, :], x_res[0:H, 1, 0:DK]
    xt_hi = sb("xt_hi", [128, NC, B, BLK], fp32r)
    xt_lo = sb("xt_lo", [128, NC, B, BLK], fp32r)
    sig = sb("sig", [128, 2, T, 4 * SEG])
    sigk = sb("sigk", [128, T, BLK])
    qraw = sb("qraw", [128, T, BLK])
    kraw = sb("kraw", [128, T, BLK])
    ex = sb("ex", [128, T, BLK])
    val_sb = sb("val_sb", [128, B, HG, DK])
    ksig = sb("ksig", [128, T, DK])
    sm = sb("sm", [128, T, SEG])
    smx = sb("smx", [128, T])
    ssum = sb("ssum", [128, T])
    sinv = sb("sinv", [128, T])
    pd = sb("pd", [128, T, BLK])
    pt = sb("pt", [128, T, BLK])
    cs = sb("cs", [128, T, BLK])
    am = sb("am", [128, 2, T, DK])
    att = sb("att", [128, B * PIECES, BLK])
    dl = [sb(f"dl{g}", [128, T, ZC]) for g in range(2)]
    rden = sb("rden", [128, HG, 2, B])
    mask = sb("mask", [128, SEG])
    ident = sb("ident", [128, 128])
    by_piece = sb("by_piece", [128, 128])
    by_piece_swapped = sb("by_piece_swapped", [128, 128])
    bt = sb("bt", [128, 4, H])
    beta, omb = bt[:, 2, :], bt[:, 3, :]
    ln_x, ln_x1 = [{part: sb(f"{part}_{of}", [128, B] + width) for part, width in
                    (("st", [6]), ("mv", [2]), ("v", []), ("rs", []), ("a", []), ("b", []))}
                   for of in ("x", "x1")]
    x1 = sb("x1", [128, B, D])
    xrow = sb("xrow", [128, B, ROW])
    x1t = sb("x1t", [128, NC, B, BLK])
    zero = sb("zero", [128, ZEROS])
    gwt = sb("gwt", [128, NC, E])
    gbias = sb("gbias", [128, B, E])
    eg = sb("eg", [128, B, E])
    score = sb("score", [128, B, E])
    scb = sb("scb", [128, B, E])
    g8 = sb("g8", [128, B, GR, 8])
    gsx = sb("gsx", [128, B, 10])
    gtop = sb("gtop", [128, B, 8])
    glist = sb("glist", [128, B, 8])
    grp = sb("grp", [128, B, 10])
    gm = sb("gm", [128, B, GR])
    tmpa = sb("tmpa", [128, B, E])
    tmpx = sb("tmpx", [128, B, E + 4])
    ttop = sb("ttop", [128, B, 8])
    tlist = sb("tlist", [128, B, 8])
    trp = sb("trp", [128, B, E + 4])
    pick = sb("pick", [128, B, E])
    wsel = sb("wsel", [128, B, E])
    wsum = sb("wsum", [128, 3, B])
    desc = sb("desc", [E, B, BLK])
    pickv = sb("pickv", [E, B, BLK])

    def bank(name):
        return ctx.enter_context(nc.psum_tensor(name, [128, 512], fp32))
    chain = [bank("chain0"), bank("chain1")]
    bank_o = bank("bank_o")
    bank_q, bank_k, bank_v = bank("bank_q"), bank("bank_k"), bank("bank_v")
    bank_a, bank_s = bank("bank_a"), bank("bank_s")

    names = ("w_arrived w_hi_done w_lo_done wo_arrived bt_arrived bt_ready ident_ready "
             "gw_arrived gwt_mm gwt_ready gb_arrived const_ready zero_ready zeroed desc_ready "
             "x_arrived xres_arrived x_normed xt_mm xt_hi_ready xt_lo_ready "
             "q_mm k_mm v_mm s_mm kt_mm pt_mm ct_mm at_mm wo_mm "
             "q_raw q_exp q_neg q_sig k_raw k_exp k_neg k_sig k_placed v_ready ksig_ready "
             "s_masked s_max s_shifted s_exp s_sum s_inv p_half p_ready pt_ready "
             "cs_ready att_ready "
             "x1_ready x1_normed x1_stored x1t_mm x1t_ready x1t_stored lg_mm lg_exp "
             "row_stored pickt_mm pickv_ready pickv_stored ln1_step ln2_step gate_step "
             "bt_step dve_noted").split()
    s = {n: sem(n) for n in names}
    num_mm = [sem(f"num_mm{j}") for j in range(HG)]
    upd_mm = [sem(f"upd_mm{j}") for j in range(HG)]
    den_inv = [sem(f"den_inv{j}") for j in range(HG)]
    dl_ready = [sem(f"dl_ready{j}") for j in range(HG)]
    am_ready = [sem(f"am_ready{j}") for j in range(HG)]
    mem_ready = [sem(f"mem_ready{j}") for j in range(HG)]

    SROWS = [slice(0, SEG), slice(SEG, BLK)]
    OTHER = [slice(SEG, BLK), slice(0, SEG)]
    GATE_STEPS, PICK_STEP, STATS_STEPS, NEWTONS = 20, 15, 5, 3
    LN_STEPS = STATS_STEPS + 3 * NEWTONS

    def blocks(eng, body):
        body(0, True, False)
        with eng.Fori(1, NBLK - 1) as blk:
            body(blk, False, False)
        body(NBLK - 1, False, True)

    block = ctx.enter_context(nc.Block())

    @block.sync
    def _(sp):
        def load_w(g):
            if g:
                sp.wait_ge(s["w_lo_done"], g)
            for m in range(3):
                w = io[("Wq", "Wk", "Wv")[m]].rearrange("(c p) n -> p c n", p=128)
                sp.dma_start(w_in[:, m, :, :], w[:, :, g * HG * DK:(g + 1) * HG * DK]
                             ).then_inc(s["w_arrived"], 16)

        x_blocks = io["x"].rearrange("b (n p) d -> n p b d", p=BLK)

        sp.dma_start(x_in[:, :, :], x_blocks[0]).then_inc(s["x_arrived"], 16)
        load_w(0)
        sp.dma_start(gw, io["gate_w"]).then_inc(s["gw_arrived"], 16)
        load_w(1)
        sp.dma_start(wo[:, :, :], io["Wo"].rearrange("(h p) n -> p h n", p=128)
                     ).then_inc(s["wo_arrived"], 16)
        sp.dma_start(gbias[:, :, :], io["gate_bias"].unsqueeze(0).unsqueeze(0)
                     .to_broadcast([128, B, E])).then_inc(s["gb_arrived"], 16)

        def body(blk, first, last):
            if not last:
                sp.wait_ge(s["xt_mm"], blk + 1)
                nxt = x_blocks[bass.ds(blk + 1, 1)] if not first else x_blocks[1:2]
                sp.dma_start(x_in[:, :, :], nxt.rearrange("n p b d -> p (n b) d")
                             ).then_inc(s["x_arrived"], 16)
            if first:
                for g in range(2, NG):
                    load_w(g)
            else:
                store_x1(blk)
            load_res(blk)
            zero_part(blk)
            if first:
                spare = scratch["rows"][N:N + CAP, :].rearrange("n d -> (n d)").rearrange(
                    "(p k m) -> p k m", p=128, k=2)
                sp.dma_start(spare, zero[:, 0:spare.shape[2]].unsqueeze(1)
                             .to_broadcast([128, 2, spare.shape[2]])).then_inc(s["zeroed"], 16)
            else:
                store_rest(blk)

        def zero_part(blk):
            if isinstance(blk, int) and blk == 0:
                sp.wait_ge(s["zero_ready"], 1)
            part = (scratch["y_parts"][blk:blk + 1] if isinstance(blk, int)
                    else scratch["y_parts"][bass.ds(blk, 1)])
            sp.dma_start(part.rearrange("n p (k m) -> p (n k) m", m=ZEROS),
                         zero[:, :].unsqueeze(1).to_broadcast([128, YPART // ZEROS, ZEROS])
                         ).then_inc(s["zeroed"], 16)

        def load_res(blk):
            if isinstance(blk, int) and blk == 0:
                sp.wait_ge(s["gwt_mm"], 1)
            cur = (x_blocks[blk:blk + 1] if isinstance(blk, int) else x_blocks[bass.ds(blk, 1)])
            cur = cur.rearrange("n p b d -> p (n b) d")
            sp.dma_start(x_res[:, :, :], cur).then_inc(s["xres_arrived"], 16)

        def at(ap, blk):
            return ap[blk - 1:blk] if isinstance(blk, int) else ap[bass.ds(blk - 1, 1)]

        def store_x1(blk):
            sp.wait_ge(s["x1_ready"], blk)
            sp.dma_start(at(scratch["x1"], blk).rearrange("n p d -> p (n d)"),
                         x1[:, :, :].rearrange("p b d -> p (b d)")).then_inc(s["x1_stored"], 16)

        def store_rest(blk):
            sp.wait_ge(s["x1t_ready"], blk)
            sp.dma_start(at(scratch["x1t"], blk).rearrange("n p d -> p (n d)"),
                         x1t[:, :, :, :].rearrange("p c b t -> p (c b t)")
                         ).then_inc(s["x1t_stored"], 16)
            sp.wait_ge(s["gate_step"], GATE_STEPS * blk)
            rows = scratch["rows"][0:N, :].rearrange("(b n p) d -> n p b d", b=B, p=BLK)
            rows = at(rows, blk).rearrange("n p b d -> p (n b) d")
            sp.dma_start(rows, xrow[:, :, :]).then_inc(s["row_stored"], 16)
            sp.wait_ge(s["pickv_ready"], blk + 1)
            picks = scratch["picks"].rearrange("e (b n t) -> n e b t", b=B, t=BLK)
            sp.dma_start(at(picks, blk).rearrange("n e b t -> e (n b) t"), pickv[:, :, :]
                         ).then_inc(s["pickv_stored"], 16)

        blocks(sp, body)
        store_x1(NBLK)
        store_rest(NBLK)
        sp.wait_ge(s["zeroed"], 16 * (NBLK + 1))
        sp.wait_ge(s["x1_stored"], 16 * (NBLK + 1))
        sp.wait_ge(s["x1t_stored"], 16 * NBLK)
        sp.wait_ge(s["row_stored"], 16 * (NBLK + 1))
        sp.wait_ge(s["pickv_stored"], 16 * (NBLK + 1))

    @block.gpsimd
    def _(pool):
        nc.gpsimd.memset(ident[:, :], 0.0).then_inc(s["ident_ready"], 1)
        pool.wait_ge(s["ident_ready"], 1)
        nc.gpsimd.affine_select(out=ident[:, :], in_=ident[:, :], compare_op=ALU.not_equal,
                                fill=1.0, base=0, pattern=[[-1, 128]], channel_multiplier=1
                                ).then_inc(s["ident_ready"], 1)
        nc.gpsimd.memset(by_piece[:, :], 0.0).then_inc(s["ident_ready"], 1)
        nc.gpsimd.memset(by_piece_swapped[:, :], 0.0).then_inc(s["ident_ready"], 1)
        pool.wait_ge(s["ident_ready"], 4)
        for m, base, seg_step in ((by_piece, 0, -SEG), (by_piece_swapped, -SEG, SEG)):
            nc.gpsimd.affine_select(out=m[:, :], in_=m[:, :],
                                    compare_op=ALU.not_equal, fill=1.0, base=base,
                                    pattern=[[-1, PIECES], [seg_step, 2], [-PIECES, QR]],
                                    channel_multiplier=1).then_inc(s["ident_ready"], 1)
        pool.wait_ge(s["ident_ready"], 6)
        nc.gpsimd.memset(mask[:, :], 0.0).then_inc(s["const_ready"], 1)
        pool.wait_ge(s["const_ready"], 1)
        for half in range(2):
            rows = slice(SEG * half, SEG * half + SEG)
            nc.gpsimd.affine_select(out=mask[rows, :], in_=mask[rows, :], compare_op=ALU.is_ge,
                                    fill=MASKED, base=0, pattern=[[-1, SEG]],
                                    channel_multiplier=1).then_inc(s["const_ready"], 1)
            pool.wait_ge(s["const_ready"], 2 + half)
        nc.gpsimd.memset(pd[:, :, :], 0.0).then_inc(s["const_ready"], 1)
        nc.gpsimd.iota(desc[:, :, :], pattern=[[-S, B], [-1, BLK]], base=N, channel_multiplier=0,
                       allow_small_or_imprecise_dtypes=True).then_inc(s["desc_ready"], 1)
        pool.wait_ge(s["const_ready"], 4)

        def step(n, first=False):
            pool.wait_ge(s["s_max"], n + 1)
            nc.gpsimd.tensor_tensor(sm[:, :, :], sm[:, :, :],
                                    smx[:, :].unsqueeze(2).to_broadcast([128, T, SEG]),
                                    ALU.subtract).then_inc(s["s_shifted"], 1)
            pool.wait_ge(s["s_inv"], n + 1)
            if not first:
                pool.wait_ge(s["pt_mm"], n)
            for seg in range(2):
                r = SROWS[seg]
                if seg:
                    pool.wait_ge(s["p_half"], n + 1)
                ins = nc.gpsimd.tensor_tensor(pd[r, :, r], sm[r, :, :],
                                              sinv[r, :].unsqueeze(2).to_broadcast([SEG, T, SEG]),
                                              ALU.mult
                                              ).then_inc(s[("p_half", "p_ready")[seg]], 1)
            pool.wait_ge(s["p_ready"], n + 1)

        step(0, True)
        with pool.Fori(1, NBLK * NG) as n:
            step(n)

    @block.scalar
    def _(act):
        act.dma_start(betas, io["betas"].rearrange("a h b d -> (a h b) d")
                      ).then_inc(s["bt_arrived"], 16)

        def split_hi(g):
            act.wait_ge(s["w_arrived"], 48 * (g + 1))
            nc.scalar.activation(w_hi[:, g, :, :, :], w_in[:, :, :, :], ACT.Copy
                                 ).then_inc(s["w_hi_done"], 1)

        def xt_hi_part(count):
            act.wait_ge(s["xt_mm"], count)
            nc.scalar.activation(xt_hi[:, :, :, :].rearrange("p c b t -> p (c b t)"), bank_a[:, :],
                                 ACT.Copy).then_inc(s["xt_hi_ready"], 1)

        def queries(n, first_ever=False):
            act.wait_ge(s["q_mm"], n + 1)
            if not first_ever:
                act.wait_ge(s["s_mm"], n)
            nc.scalar.activation(qraw[:, :, :], bank_q[:, :], ACT.Copy).then_inc(s["q_raw"], 1)
            if not first_ever:
                act.wait_ge(s["k_sig"], n)
            nc.scalar.activation(ex[:, :, :], bank_q[:, :], ACT.Relu, scale=-1.0
                                 ).then_inc(s["q_neg"], 1)
            act.wait_ge(s["q_neg"], n + 1)
            nc.scalar.activation(ex[:, :, :], ex[:, :, :], ACT.Exp, scale=-1.0
                                 ).then_inc(s["q_exp"], 1)

        def keys(n):
            act.wait_ge(s["k_mm"], n + 1)
            nc.scalar.activation(kraw[:, :, :], bank_k[:, :], ACT.Copy).then_inc(s["k_raw"], 1)

        def keys_exp(n):
            act.wait_ge(s["q_sig"], n + 1)
            nc.scalar.activation(ex[:, :, :], bank_k[:, :], ACT.Relu, scale=-1.0
                                 ).then_inc(s["k_neg"], 1)
            act.wait_ge(s["k_neg"], n + 1)
            nc.scalar.activation(ex[:, :, :], ex[:, :, :], ACT.Exp, scale=-1.0
                                 ).then_inc(s["k_exp"], 1)

        def place_keys(n, par):
            act.wait_ge(s["k_sig"], n + 1)
            for seg in range(2):
                ins = nc.scalar.activation(sig[:, par, :, 3 * SEG * seg:3 * SEG * seg + SEG],
                                           sigk[:, :, SROWS[seg]], ACT.Copy)
            ins.then_inc(s["k_placed"], 1)

        def values(n):
            act.wait_ge(s["v_mm"], n + 1)
            nc.scalar.activation(val_sb[:, :, :, :], bank_v[:, :], ACT.Copy
                                 ).then_inc(s["v_ready"], 1)

        def key_rows(n):
            act.wait_ge(s["kt_mm"], n + 1)
            nc.scalar.activation(ksig[:, :, :], bank_k[:, :], ACT.Copy
                                 ).then_inc(s["ksig_ready"], 1)

        def read_out(n, g, seg, j):
            act.wait_ge(den_inv[j], 2 * n + seg + 1)
            r = OTHER[seg]
            for b in range(B):
                ins = nc.scalar.activation(am[r, g % 2, j * B + b, :],
                                           chain[j][r, b * ZC:b * ZC + DK], ACT.Copy,
                                           scale=rden[r, j, seg, b:b + 1])
            ins.then_inc(am_ready[j], 1)

        split_hi(0)
        xt_hi_part(1)
        act.wait_ge(s["gwt_mm"], 1)
        nc.scalar.activation(bt[:, 1, :], bank_s[:, NC * E:NC * E + H], ACT.Exp, scale=-1.0
                             ).then_inc(s["bt_step"], 1)
        nc.scalar.activation(gwt[:, :, :], bank_s[:, 0:NC * E], ACT.Copy
                             ).then_inc(s["gwt_ready"], 1)
        split_hi(1)
        queries(0, True)
        keys(0)
        keys_exp(0)
        place_keys(0, 0)
        values(0)
        key_rows(0)
        act.wait_ge(s["bt_ready"], 1)

        def body(blk, first, last):
            for g in range(NG):
                n = blk * NG + g
                nxt = not (last and g == NG - 1)
                if not (first and g < 2):
                    act.wait_ge(s["at_mm"], n - 1)
                read_out(n, g, 0, 0)
                read_out(n, g, 0, 1)
                act.wait_ge(s["s_shifted"], n + 1)
                nc.scalar.activation(sm[:, :, :], sm[:, :, :], ACT.Exp, scale=KSCALE
                                     ).then_inc(s["s_exp"], 1)
                if nxt:
                    queries(n + 1)
                if nxt:
                    keys(n + 1)
                read_out(n, g, 1, 0)
                act.wait_ge(s["pt_mm"], n + 1)
                nc.scalar.activation(pt[:, :, :], bank_v[:, :], ACT.Copy).then_inc(s["pt_ready"], 1)
                read_out(n, g, 1, 1)
                if nxt:
                    keys_exp(n + 1)
                act.wait_ge(s["ct_mm"], n + 1)
                if not (first and g == 0):
                    act.wait_ge(s["att_ready"], 2 * n)
                for j in range(HG):
                    nc.scalar.activation(cs[:, j * B:j * B + B, :],
                                         bank_q[:, j * B * BLK:(j + 1) * B * BLK], ACT.Copy,
                                         scale=omb[:, HG * g + j:HG * g + j + 1]
                                         ).then_inc(s["cs_ready"], 1)
                if first and g + 2 < NG:
                    split_hi(g + 2)
                if nxt:
                    place_keys(n + 1, (g + 1) % 2)
                if nxt:
                    values(n + 1)
                if g == 3 and not first:
                    side_x1t(blk)
                if g == 4 and not first:
                    logits_exp(blk)
                if g == NG - 1 and not first:
                    act.wait_ge(s["x1t_stored"], 16 * blk)
                if g == NG - 2 and not last:
                    act.wait_ge(s["v_mm"], n + 2)
                    xt_hi_part(blk + 2)
                if nxt:
                    key_rows(n + 1)

        def logits_exp(blk):
            act.wait_ge(s["lg_mm"], blk)
            nc.scalar.activation(eg[:, :, :], bank_a[:, 0:B * E], ACT.Exp, scale=-1.0
                                 ).then_inc(s["lg_exp"], 1)

        def side_x1t(blk):
            act.wait_ge(s["x1t_mm"], blk)
            nc.scalar.activation(x1t[:, :, :, :].rearrange("p c b t -> p (c b t)"), bank_a[:, :],
                                 ACT.Copy).then_inc(s["x1t_ready"], 1)

        blocks(act, body)
        side_x1t(NBLK)
        logits_exp(NBLK)

    @block.vector
    def _(dve):
        def split_lo(g):
            dve.wait_ge(s["w_hi_done"], g + 1)
            nc.vector.tensor_tensor(w_lo[:, g, :, :, :].rearrange("p m c n -> p (m c n)"),
                                    w_in[:, :, :, :].rearrange("p m c n -> p (m c n)"),
                                    w_hi[:, g, :, :, :].rearrange("p m c n -> p (m c n)")
                                    .bitcast(fp32), ALU.subtract).then_inc(s["w_lo_done"], 1)

        def norm_stats(w, x_t, done, base):
            st, mv, v, half, guess = w["st"], w["mv"], w["v"], w["a"], w["rs"]
            link = link_on(dve, s[done], base, s["dve_noted"])
            for b in range(B):
                ins = nc.vector.bn_stats(out=st[:, b, :], in_=x_t[:, b, :])
            link(ins, alone=True)
            for b in range(B):
                ins = nc.vector.bn_aggr(out=mv[:, b, :], in_=st[:, b, :])
            link(ins)
            link(nc.vector.tensor_scalar_add(v[:, :], mv[:, :, 1], LN_EPS))
            link(nc.vector.tensor_single_scalar(half[:, :].bitcast(i32), v[:, :].bitcast(i32),
                                                1, ALU.logical_shift_right))
            link(nc.vector.tensor_scalar(guess[:, :].bitcast(i32), half[:, :].bitcast(i32), -1.0,
                                         RSQRT_MAGIC, ALU.mult, ALU.add))

        def norm_newton(w, rounds, done, base):
            v, a, b, rs = w["v"], w["a"], w["b"], w["rs"]
            link = link_on(dve, s[done], base)
            for _ in range(rounds):
                link(nc.vector.tensor_tensor(a[:, :], rs[:, :], rs[:, :], ALU.mult))
                link(nc.vector.scalar_tensor_tensor(out=b[:, :], in0=a[:, :], scalar=-0.5,
                                                    in1=v[:, :], op0=ALU.mult, op1=ALU.mult))
                link(nc.vector.scalar_tensor_tensor(out=rs[:, :], in0=b[:, :], scalar=1.5,
                                                    in1=rs[:, :], op0=ALU.add, op1=ALU.mult))

        def norm_apply(w, out, x_t, done):
            for b in range(B):
                ins = nc.vector.tensor_scalar(out[:, b, 0:D], x_t[:, b, :], w["mv"][:, b, 0:1],
                                              w["rs"][:, b:b + 1], ALU.subtract, ALU.mult)
            ins.then_inc(s[done], 1)

        def x_stats(count):
            dve.wait_ge(s["x_arrived"], 16 * count)
            norm_stats(ln_x, x_in, "ln1_step", (count - 1) * LN_STEPS)

        def x_newton(count, first_round, rounds):
            norm_newton(ln_x, rounds, "ln1_step",
                        (count - 1) * LN_STEPS + STATS_STEPS + 3 * first_round)

        def x_apply():
            norm_apply(ln_x, x_in, x_in, "x_normed")

        def xt_lo_part(count):
            dve.wait_ge(s["xt_hi_ready"], count)
            nc.vector.tensor_tensor(xt_lo[:, :, :, :].rearrange("p c b t -> p (c b t)"),
                                    bank_a[:, :],
                                    xt_hi[:, :, :, :].rearrange("p c b t -> p (c b t)")
                                    .bitcast(fp32), ALU.subtract).then_inc(s["xt_lo_ready"], 1)

        def sigma_q(n, par):
            dve.wait_ge(s["q_exp"], n + 1)
            nc.vector.scalar_tensor_tensor(
                out=sig[:, par, :, SEG:3 * SEG],
                in0=bank_q[:, :].rearrange("p (t c) -> p t c", t=T), scalar=0.0,
                in1=ex[:, :, :], op0=ALU.max, op1=ALU.add).then_inc(s["q_sig"], 1)

        def sigma_k(n, par):
            dve.wait_ge(s["k_exp"], n + 1)
            if not (isinstance(n, int) and n == 0):
                dve.wait_ge(s["kt_mm"], n)
            nc.vector.scalar_tensor_tensor(
                out=sigk[:, :, :], in0=bank_k[:, :].rearrange("p (t c) -> p t c", t=T),
                scalar=0.0, in1=ex[:, :, :], op0=ALU.max, op1=ALU.add).then_inc(s["k_sig"], 1)

        def delta(n, seg):
            if seg == 0:
                dve.wait_ge(s["v_ready"], n + 1)
            for j in range(HG):
                dve.wait_ge(num_mm[j], 2 * n + seg + 1)
                nc.vector.reciprocal(rden[:, j, seg, :],
                                     chain[j][:, DK:DK + ZC + 1:ZC]).then_inc(den_inv[j], 1)
                dve.wait_ge(den_inv[j], 2 * n + seg + 1)
                r = SROWS[seg]
                for b in range(B):
                    ins = nc.vector.scalar_tensor_tensor(
                        out=dl[seg][r, j * B + b, 0:DK], in0=chain[j][r, b * ZC:b * ZC + DK],
                        scalar=rden[r, j, seg, b:b + 1], in1=val_sb[r, b, j, :],
                        op0=ALU.mult, op1=ALU.subtract)
                ins.then_inc(dl_ready[j], 1)

        def state(n, g, seg):
            for j in range(HG):
                dve.wait_ge(upd_mm[j], 2 * n + seg + 1)
                m = mem[:, HG * g + j, :, :].rearrange("p b z -> p (b z)")
                nc.vector.tensor_tensor(m, m, chain[j][:, 0:B * ZC], ALU.subtract
                                        ).then_inc(mem_ready[j], 1)

        def attend(n, g, blk):
            dve.wait_ge(s["at_mm"], n + 1)
            dve.wait_ge(s["cs_ready"], 2 * n + 2)
            if g == 0 and not (isinstance(n, int) and n == 0):
                dve.wait_ge(s["wo_mm"], blk)
            for j in range(HG):
                h = HG * g + j
                read = bank_a[:, j * B * BLK:(j + 1) * B * BLK].rearrange(
                    "p (a s q) -> p a s q", s=2, q=QR)
                soft = cs[:, j * B:j * B + B, :].rearrange("p b (a s q) -> p (b a) s q", s=2, q=QR)
                for seg in range(2):
                    c = seg * SEG + h * QR
                    ins = nc.vector.scalar_tensor_tensor(
                        out=att[:, :, c:c + QR], in0=read[:, :, seg, :], scalar=beta[:, h:h + 1],
                        in1=soft[:, :, seg, :], op0=ALU.mult, op1=ALU.add)
                ins.then_inc(s["att_ready"], 1)

        def residual(blk):
            dve.wait_ge(s["wo_mm"], blk)
            dve.wait_ge(s["x1_stored"], 16 * blk)
            dve.wait_ge(s["xres_arrived"], 16 * blk)
            nc.vector.tensor_tensor(x1[:, :, :].rearrange("p b d -> p (b d)"), bank_o[:, :],
                                    x_res[:, :, :].rearrange("p b d -> p (b d)"), ALU.add
                                    ).then_inc(s["x1_ready"], 1)

        def x1_stats(blk):
            dve.wait_ge(s["x1_ready"], blk)
            norm_stats(ln_x1, x1, "ln2_step", (blk - 1) * LN_STEPS)

        def x1_newton(blk, first_round, rounds):
            norm_newton(ln_x1, rounds, "ln2_step",
                        (blk - 1) * LN_STEPS + STATS_STEPS + 3 * first_round)

        def x1_apply(blk):
            dve.wait_ge(s["row_stored"], 16 * blk)
            norm_apply(ln_x1, xrow, x1, "x1_normed")

        def gate_link(blk, before):
            return link_on(dve, s["gate_step"], (blk - 1) * GATE_STEPS + before, s["dve_noted"])

        def gate_scores(blk):
            dve.wait_ge(s["lg_exp"], blk)
            link, v = gate_link(blk, 0), nc.vector
            link(v.tensor_scalar_add(eg[:, :, :], eg[:, :, :], 1.0))
            link(v.reciprocal(score[:, :, :], eg[:, :, :]))
            link(v.tensor_tensor(scb[:, :, :], score[:, :, :], gbias[:, :, :], ALU.add), True)

        def gate_group_sums(blk):
            link, v = gate_link(blk, 3), nc.vector
            for b in range(B):
                for i in range(GR):
                    ins = v.max(g8[:, b, i, :], scb[:, b, GE * i:GE * i + GE])
            link(ins)
            link(v.tensor_tensor(gsx[:, :, 0:GR], g8[:, :, :, 0], g8[:, :, :, 1], ALU.add), True)

        def gate_groups(blk):
            link, v = gate_link(blk, 5), nc.vector
            for b in range(B):
                ins = v.max(gtop[:, b, :], gsx[:, b, :])
            link(ins)
            link(v.tensor_copy(glist[:, :, 0:2], gtop[:, :, 0:2]), True)
            for b in range(B):
                ins = v.match_replace(out=grp[:, b, :], in_to_replace=glist[:, b, :],
                                      in_values=gsx[:, b, :], imm_value=BIG)
            link(ins)
            link(v.tensor_scalar(gm[:, :, :], grp[:, :, 0:GR], BIG, None, ALU.is_equal))

        def gate_best(blk):
            link, v = gate_link(blk, 9), nc.vector
            link(v.tensor_tensor(tmpa[:, :, :].rearrange("p b (g e) -> p b g e", g=GR),
                                 scb[:, :, :].rearrange("p b (g e) -> p b g e", g=GR),
                                 gm[:, :, :].unsqueeze(3).to_broadcast([128, B, GR, GE]), ALU.mult))
            link(v.tensor_scalar_add(tmpx[:, :, 0:E], tmpa[:, :, :], 0.0), True)
            for b in range(B):
                ins = v.max(ttop[:, b, :], tmpx[:, b, 0:E])
            link(ins)
            link(v.tensor_copy(tlist[:, :, 0:TOPK], ttop[:, :, 0:TOPK]), True)

        def gate_picks(blk):
            link, v = gate_link(blk, 13), nc.vector
            for b in range(B):
                ins = v.match_replace(out=trp[:, b, :], in_to_replace=tlist[:, b, :],
                                      in_values=tmpx[:, b, :], imm_value=BIG)
            link(ins)
            link(v.tensor_scalar(pick[:, :, :], trp[:, :, 0:E], BIG, None, ALU.is_equal))

        def gate_weights(blk):
            link, v = gate_link(blk, PICK_STEP), nc.vector
            link(v.tensor_tensor(wsel[:, :, :], score[:, :, :], pick[:, :, :], ALU.mult))
            link(v.tensor_reduce(wsum[:, 0, :], wsel[:, :, :], axis=AX.X, op=ALU.add))
            link(v.tensor_scalar_add(wsum[:, 1, :], wsum[:, 0, :], 1e-20))
            link(v.reciprocal(wsum[:, 2, :], wsum[:, 1, :]))
            for b in range(B):
                ins = v.tensor_scalar(xrow[:, b, D:ROW], wsel[:, b, :], wsum[:, 2, b:b + 1], 2.0,
                                      ALU.mult, ALU.mult)
            link(ins)

        def picks(blk):
            dve.wait_ge(s["pickt_mm"], blk)
            dve.wait_ge(s["desc_ready"], blk)
            dve.wait_ge(s["pickv_stored"], 16 * blk)
            pk = bank_a[0:E, 0:B * BLK].rearrange("p (b t) -> p b t", b=B)
            nc.vector.tensor_tensor(pickv[:, :, :], pk, desc[:, :, :], ALU.mult
                                    ).then_inc(s["pickv_ready"], 1)
            dve.wait_ge(s["pickv_ready"], blk + 1)
            nc.vector.tensor_scalar_add(desc[:, :, :], desc[:, :, :], -float(BLK)
                                        ).then_inc(s["desc_ready"], 1)

        for done, count in (("x1_stored", 16), ("row_stored", 16), ("pickv_stored", 16),
                            ("pickv_ready", 1)):
            nc.vector.sem_inc(s[done], count)
        nc.vector.memset(mem[:, :, :, 0:DK], 0.0)
        nc.vector.memset(mem[:, :, :, DK:ZC], 1.0 / DK)
        for seg in range(2):
            nc.vector.memset(dl[seg][OTHER[seg], :, :], 0.0)
            nc.vector.memset(dl[seg][SROWS[seg], :, DK:ZC], -1.0)
        nc.vector.memset(gsx[:, :, :], SENT)
        nc.vector.memset(glist[:, :, :], SENT)
        nc.vector.memset(tmpx[:, :, :], SENT)
        nc.vector.memset(tlist[:, :, :], SENT)
        nc.vector.memset(zero[:, :], 0.0).then_inc(s["zero_ready"], 1)
        dve.wait_ge(s["zero_ready"], 1)
        x_stats(1)
        x_newton(1, 0, NEWTONS)
        x_apply()
        split_lo(0)
        xt_lo_part(1)
        dve.wait_ge(s["bt_step"], 1)
        link = link_on(dve, s["bt_step"], 1)
        link(nc.vector.tensor_scalar_add(bt[:, 0, :], bt[:, 1, :], 1.0))
        link(nc.vector.reciprocal(beta, bt[:, 0, :]))
        nc.vector.tensor_scalar(omb, beta, -1.0, 1.0, ALU.mult, ALU.add).then_inc(s["bt_ready"], 1)
        split_lo(1)
        sigma_q(0, 0)
        sigma_k(0, 0)
        dve.wait_ge(s["const_ready"], 4)
        dve.wait_ge(s["gb_arrived"], 16)

        def body(blk, first, last):
            for g in range(NG):
                n = blk * NG + g
                nxt = not (last and g == NG - 1)
                dve.wait_ge(s["s_mm"], n + 1)
                for seg in range(2):
                    r = SROWS[seg]
                    ins = nc.vector.tensor_tensor(
                        sm[r, :, :], bank_s[:, :].rearrange("p (t c) -> p t c", t=T)[r, :, r],
                        mask[r, :].unsqueeze(1).to_broadcast([SEG, T, SEG]), ALU.add)
                ins.then_inc(s["s_masked"], 1)
                dve.wait_ge(s["s_masked"], n + 1)
                nc.vector.tensor_reduce(smx[:, :], sm[:, :, :], axis=AX.X, op=ALU.max
                                        ).then_inc(s["s_max"], 1)
                delta(n, 0)
                if g == 0 and not first:
                    attend(n - 1, NG - 1, blk)
                dve.wait_ge(s["s_exp"], n + 1)
                nc.vector.tensor_reduce(ssum[:, :], sm[:, :, :], axis=AX.X, op=ALU.add
                                        ).then_inc(s["s_sum"], 1)
                dve.wait_ge(s["s_sum"], n + 1)
                nc.vector.reciprocal(sinv[:, :], ssum[:, :]).then_inc(s["s_inv"], 1)
                state(n, g, 0)
                if nxt:
                    sigma_q(n + 1, (g + 1) % 2)
                delta(n, 1)
                if g:
                    attend(n - 1, g - 1, blk)
                if g == 0 and not last:
                    x_stats(blk + 2)
                if g == 1 and not first:
                    residual(blk)
                if g == 2 and not first:
                    x1_newton(blk, 0, 1)
                if g == 3 and not first:
                    x1_apply(blk)
                if g == 4 and not last:
                    x_apply()
                if g == 5 and not first:
                    gate_scores(blk)
                if g == 6 and not first:
                    gate_groups(blk)
                if g == 7 and not first:
                    gate_picks(blk)
                if nxt:
                    sigma_k(n + 1, (g + 1) % 2)
                state(n, g, 1)
                if g == 0 and not last:
                    x_newton(blk + 2, 0, 1)
                if g == 1 and not first:
                    x1_stats(blk)
                if g == 2 and not first:
                    x1_newton(blk, 1, 2)
                if g == 3 and not last:
                    x_newton(blk + 2, 1, 2)
                if g == 5 and not first:
                    gate_group_sums(blk)
                if g == 6 and not first:
                    gate_best(blk)
                if g == 7 and not first:
                    gate_weights(blk)
                    picks(blk)
                if first and g + 2 < NG:
                    split_lo(g + 2)
                if g == NG - 2 and not last:
                    dve.wait_ge(s["v_mm"], n + 2)
                    xt_lo_part(blk + 2)

        blocks(dve, body)
        attend(NBLK * NG - 1, NG - 1, None)
        residual(NBLK)
        x1_stats(NBLK)
        x1_newton(NBLK, 0, NEWTONS)
        x1_apply(NBLK)
        gate_scores(NBLK)
        gate_group_sums(NBLK)
        gate_groups(NBLK)
        gate_best(NBLK)
        gate_picks(NBLK)
        gate_weights(NBLK)
        picks(NBLK)

    @block.tensor
    def _(pe):
        mm = nc.tensor.matmul

        def x_transposes():
            for c in range(NC):
                for b in range(B):
                    ins = nc.tensor.transpose(bank_a[:, (c * B + b) * BLK:(c * B + b + 1) * BLK],
                                              x_in[:, b, c * 128:(c + 1) * 128], ident[:, :])
            ins.then_inc(s["xt_mm"], 1)

        def project_t(out_bank, g, m, heads=range(HG)):
            for j in heads:
                out = out_bank[:, j * B * BLK:(j + 1) * B * BLK]
                col = slice(j * DK, (j + 1) * DK)
                parts = [(w, x, c) for w, x in ((w_hi, xt_hi), (w_hi, xt_lo), (w_lo, xt_hi))
                         for c in range(NC)]
                for i, (w, x, c) in enumerate(parts):
                    ins = mm(out, w[:, g, m, c, col], x[:, c, :, :].rearrange("p b t -> p (b t)"),
                             start=i == 0, stop=i == len(parts) - 1)
            return ins

        def project_v(g):
            for b in range(B):
                out = bank_v[:, b * HG * DK:(b + 1) * HG * DK]
                parts = [(w, x, c) for w, x in ((w_hi, xt_hi), (w_hi, xt_lo), (w_lo, xt_hi))
                         for c in range(NC)]
                for i, (w, x, c) in enumerate(parts):
                    ins = mm(out, x[:, c, b, :], w[:, g, 2, c, :],
                             start=i == 0, stop=i == len(parts) - 1)
            return ins

        def scores(n, first_ever):
            pe.wait_ge(s["k_raw"], n + 1)
            pe.wait_ge(s["q_raw"], n + 1)
            if not first_ever:
                pe.wait_ge(s["s_masked"], n)
            for t in range(T):
                ins = mm(bank_s[:, t * BLK:(t + 1) * BLK],
                         qraw[:, t, :], kraw[:, t, :], start=True, stop=True)
            ins.then_inc(s["s_mm"], 1)

        def key_transposes(n):
            pe.wait_ge(s["k_sig"], n + 1)
            for t in range(T):
                ins = nc.tensor.transpose(bank_k[:, t * DK:(t + 1) * DK], sigk[:, t, :],
                                          ident[:, :])
            ins.then_inc(s["kt_mm"], 1)

        def numerators(n, g, seg):
            for j in range(HG):
                if not (isinstance(n, int) and n == 0 and seg == 0):
                    pe.wait_ge(mem_ready[j], 2 * n + seg)
                for b in range(B):
                    ins = mm(chain[j][:, b * ZC:(b + 1) * ZC],
                             sig[:, g % 2, j * B + b, seg * BLK:(seg + 1) * BLK],
                             mem[:, HG * g + j, b, :], start=True, stop=True)
                ins.then_inc(num_mm[j], 1)

        def update(n, seg, j):
            pe.wait_ge(dl_ready[j], 2 * n + seg + 1)
            pe.wait_ge(am_ready[j], 2 * n + seg + 1)
            for b in range(B):
                ins = mm(chain[j][:, b * ZC:(b + 1) * ZC], ksig[:, j * B + b, :],
                         dl[seg][:, j * B + b, :], start=True, stop=True)
            ins.then_inc(upd_mm[j], 1)

        def read_transposes(n, par):
            pe.wait_ge(am_ready[0], 2 * n + 2)
            pe.wait_ge(am_ready[1], 2 * n + 2)
            for t in range(T):
                ins = nc.tensor.transpose(bank_a[:, t * BLK:(t + 1) * BLK], am[:, par, t, :],
                                          by_piece_swapped[:, :])
            ins.then_inc(s["at_mm"], 1)

        def project_out(lo, hi, n=None):
            if lo == 0:
                pe.wait_ge(s["att_ready"], 2 * n)
            for i in range(lo, hi):
                for b in range(B):
                    ins = mm(bank_o[:, b * D:(b + 1) * D], att[:, b * PIECES + i, :], wo[:, i, :],
                             start=(i == 0 and b == 0), stop=(i == PIECES - 1),
                             skip_group_check=True)
            if hi == PIECES:
                ins.then_inc(s["wo_mm"], 1)

        def x1_transposes(blk):
            pe.wait_ge(s["x1_normed"], blk)
            for c in range(NC):
                for b in range(B):
                    ins = nc.tensor.transpose(bank_a[:, (c * B + b) * BLK:(c * B + b + 1) * BLK],
                                              xrow[:, b, c * 128:(c + 1) * 128], ident[:, :])
            ins.then_inc(s["x1t_mm"], 1)

        def logits(blk):
            pe.wait_ge(s["x1t_ready"], blk)
            for b in range(B):
                for c in range(NC):
                    ins = mm(bank_a[:, b * E:(b + 1) * E], x1t[:, c, b, :], gwt[:, c, :],
                             start=c == 0, stop=c == NC - 1)
            ins.then_inc(s["lg_mm"], 1)

        def pick_transposes(blk):
            pe.wait_ge(s["gate_step"], GATE_STEPS * (blk - 1) + PICK_STEP)
            for b in range(B):
                ins = nc.tensor.transpose(bank_a[0:E, b * BLK:(b + 1) * BLK], pick[:, b, :],
                                          ident[:, :])
            ins.then_inc(s["pickt_mm"], 1)

        pe.wait_ge(s["ident_ready"], 6)
        pe.wait_ge(s["x_normed"], 1)
        x_transposes()
        pe.wait_ge(s["gw_arrived"], 16)
        for c in range(NC):
            ins = nc.tensor.transpose(bank_s[:, c * E:(c + 1) * E], gw[:, c * 128:(c + 1) * 128],
                                      ident[0:E, 0:E])
        pe.wait_ge(s["bt_arrived"], 16)
        nc.tensor.transpose(bank_s[:, NC * E:NC * E + H], betas, ident[0:H, 0:H]
                            ).then_inc(s["gwt_mm"], 1)
        pe.wait_ge(s["xt_lo_ready"], 1)
        pe.wait_ge(s["w_lo_done"], 1)
        project_t(bank_q, 0, 0).then_inc(s["q_mm"], 1)
        project_t(bank_k, 0, 1).then_inc(s["k_mm"], 1)
        project_v(0).then_inc(s["v_mm"], 1)
        pe.wait_ge(s["gwt_ready"], 1)
        scores(0, True)
        key_transposes(0)
        pe.wait_ge(s["wo_arrived"], 16)

        def body(blk, first, last):
            for g in range(NG):
                n = blk * NG + g
                gn = (g + 1) % NG
                nxt = not (last and g == NG - 1)
                pe.wait_ge(s["q_sig"], n + 1)
                pe.wait_ge(s["k_placed"], n + 1)
                numerators(n, g, 0)
                if g == 0 and not first:
                    pe.wait_ge(s["pickv_ready"], blk)
                    read_transposes(n - 1, (g - 1) % 2)
                if nxt:
                    if g == NG - 1:
                        pe.wait_ge(s["xt_lo_ready"], blk + 2)
                    if first and g + 1 < NG:
                        pe.wait_ge(s["w_lo_done"], g + 2)
                    if not (first and g == 0):
                        pe.wait_ge(s["cs_ready"], 2 * n)
                    project_t(bank_q, gn, 0).then_inc(s["q_mm"], 1)
                pe.wait_ge(s["ksig_ready"], n + 1)
                for j in range(HG):
                    update(n, 0, j)
                    if nxt:
                        ins = project_t(bank_k, gn, 1, [j])
                if nxt:
                    ins.then_inc(s["k_mm"], 1)
                if g == 0 and not first:
                    project_out(0, 6, n)
                numerators(n, g, 1)
                if g == 0 and not first:
                    project_out(6, 11)
                pe.wait_ge(s["p_ready"], n + 1)
                pe.wait_ge(s["v_ready"], n + 1)
                for t in range(T):
                    ins = nc.tensor.transpose(bank_v[:, t * BLK:(t + 1) * BLK], pd[:, t, :],
                                              by_piece[:, :])
                ins.then_inc(s["pt_mm"], 1)
                if g:
                    if not first and g == 4:
                        pe.wait_ge(s["x1t_ready"], blk)
                    if not first and g == 5:
                        pe.wait_ge(s["lg_exp"], blk)
                    read_transposes(n - 1, (g - 1) % 2)
                for j in range(HG):
                    update(n, 1, j)
                    if j == 0:
                        pe.wait_ge(s["pt_ready"], n + 1)
                        if nxt:
                            pe.wait_ge(s["q_sig"], n + 2)
                        else:
                            pe.wait_ge(s["cs_ready"], 2 * n)
                    for t in range(j * B, j * B + B):
                        ins = mm(bank_q[:, t * BLK:(t + 1) * BLK], val_sb[:, t % B, j, :],
                                 pt[:, t, :], start=True, stop=True)
                ins.then_inc(s["ct_mm"], 1)
                if g == 0 and not first:
                    project_out(11, PIECES)
                if not (first and g == 0):
                    pe.wait_ge(s["att_ready"], 2 * n)
                if g == 3 and not first:
                    x1_transposes(blk)
                if g == 4 and not first:
                    logits(blk)
                if g == NG - 2 and not last:
                    pe.wait_ge(s["x_normed"], blk + 2)
                    x_transposes()
                if g == NG - 1 and not first:
                    pick_transposes(blk)
                if nxt:
                    project_v(gn).then_inc(s["v_mm"], 1)
                    scores(n + 1, False)
                    key_transposes(n + 1)

        blocks(pe, body)
        pe.wait_ge(s["pickv_ready"], NBLK)
        read_transposes(NBLK * NG - 1, (NG - 1) % 2)
        project_out(0, PIECES, NBLK * NG)
        x1_transposes(NBLK)
        logits(NBLK)
        pick_transposes(NBLK)


def experts(nc, ctx, io, scratch, out):
    def sb(name, shape, dt=fp32):
        return ctx.enter_context(nc.sbuf_tensor(name, shape, dt))

    def sem(name):
        return ctx.enter_context(nc.semaphore(name))

    EB = 4
    NB = E // EB
    TG = 2
    NTG = NBLK // TG
    AHEAD = 4
    FC = FS // 128
    QUARTERS = N // QUART
    YB = 4

    xt = sb("xt_all", [128, NBLK, NC, B, BLK])
    acc = sb("acc", [128, NBLK, B, D])
    w13 = sb("w13", [128, E, NC, 2, F])
    w2 = sb("w2_all", [128, E, D])
    sg = sb("sg", [128, NC, FS])
    su = sb("su", [128, NC, FS])
    sd = sb("sd", [128, FC, D])
    id2 = sb("id2", [64, 64])
    vq = sb("vq", [128, QUART])
    cand = sb("cand", [128, CAP])
    cm = sb("cm", [E, QUARTERS, CAP])
    sel = sb("sel", [E, CAP])
    spare = sb("spare", [E, CAP])
    idxf = sb("idxf", [E, 3, CAP])
    idx = sb("idx", [CAP, E], u32)
    ic = sb("ic", [CAP, 2, EB], u32)
    oc = sb("oc", [CAP, 2, EB], u32)
    rows = sb("rows_in", [CAP, 2, EB, ROW])
    wc = sb("wc", [CAP, 2, EB])
    rt = sb("rt", [128, EB, NC, CAP])
    hs = sb("hs", [CAP, EB, F])
    hh = sb("hh", [CAP, EB, F])
    ht = sb("ht", [128, EB, CAP])
    ys = sb("ys", [CAP, 2, EB, D])
    sil = sb("sil", [128, FC, TG * B * BLK])
    sh = sb("sh", [128, FC, TG * B * BLK])

    def bank(name):
        return ctx.enter_context(nc.psum_tensor(name, [128, 512], fp32))
    bank_g = [bank("bank_g0"), bank("bank_g1")]
    bank_u = [bank("bank_u0"), bank("bank_u1")]
    bank_d = bank("bank_d")
    bank_t = bank("bank_t")
    bank_h = [bank("bank_h0"), bank("bank_h1")]

    names = ("vq_arrived cm_arrived shared_arrived id_ready spare_ready "
             "top_step sel_mm idx_ready g_mm u_mm sil_ready sh_ready d_mm acc_ready "
             "idx_copied out_copied added t_mm rt_ready h_mm silu_ready hh_ready ht_mm ht_ready "
             "y_mm ys_ready "
             "wc_ready out_ready out_stored pool_noted pe_noted").split()
    s = {n: sem("p2_" + n) for n in names}
    we_arrived = [sem(f"we_arrived{i}") for i in range(2)]
    gathered = [sem(f"gathered{i}") for i in range(2)]
    xt_arrived = [sem(f"xt_arrived{k}") for k in range(NBLK // YB)]
    acc_arrived = [sem(f"acc_arrived{k}") for k in range(NBLK // YB)]
    y_sems = [sem(f"y_arrived{k}") for k in range(NBLK // YB)]
    ROUNDS = CAP // 8

    def batches(eng, batch):
        for i in range(2):
            batch(i, i, i + AHEAD)
        with eng.Fori(1, (NTG - AHEAD) // 2) as pair:
            for par in range(2):
                batch(2 * pair + par, par, 2 * pair + par + AHEAD)
        for i in range(NTG - AHEAD, NB):
            batch(i, i % 2, None)

    block = ctx.enter_context(nc.Block())

    @block.sync
    def _(sp):
        for q in range(QUARTERS):
            sp.dma_start(vq[q * E:(q + 1) * E, :], scratch["picks"][:, q * QUART:(q + 1) * QUART]
                         ).then_inc(s["vq_arrived"], 16)

        def load_blocks(t, n, k, done):
            r = slice(k * YB, (k + 1) * YB)
            sp.dma_start(t[:, r].rearrange("p n a b c -> p n (a b c)" if len(t.shape) == 5 else
                                           "p n b d -> p n (b d)"),
                         scratch[n][r].rearrange("n p d -> p n d")).then_inc(done[k], 16)

        load_blocks(xt, "x1t", 0, xt_arrived)
        load_blocks(acc, "x1", 0, acc_arrived)
        load_blocks(xt, "x1t", 1, xt_arrived)

        def load_batch(i, par):
            e = slice(i * EB, (i + 1) * EB) if isinstance(i, int) else bass.ds(i * EB, EB)
            for which, n in enumerate(("w1", "w3")):
                sp.dma_start(w13[:, e, :, which, :].rearrange("p e c f -> p (e c) f"),
                             io[n][e].rearrange("e (c p) f -> p (e c) f", p=128)
                             ).then_inc(we_arrived[par], 16)
            sp.dma_start(w2[:, e, :], io["w2"][e].rearrange("e p d -> p e d")
                         ).then_inc(we_arrived[par], 16)

        sp.wait_ge(s["top_step"], 2 * ROUNDS)
        for q in range(QUARTERS):
            sp.dma_start(cm[:, q, :], cand[q * E:(q + 1) * E, :]).then_inc(s["cm_arrived"], 16)
        load_batch(0, 0)
        load_blocks(acc, "x1", 1, acc_arrived)
        load_batch(1, 1)
        for k in range(2, NBLK // YB):
            load_blocks(xt, "x1t", k, xt_arrived)
            load_blocks(acc, "x1", k, acc_arrived)
        with sp.Fori(1, NB // 2) as pair:
            for par in range(2):
                sp.wait_ge(we_arrived[par], 48 * pair)
                load_batch(2 * pair + par, par)
        sp.wait_ge(s["added"], 16 * E)
        sp.wait_ge(s["d_mm"], TG * NTG)
        y = scratch["y"][0:N, :].rearrange("(b n p) d -> p n b d", b=B, p=BLK)
        yt = xt[:, :, :, :, :].rearrange("p n c b t -> p n (c b t)").rearrange(
            "p n (b d) -> p n b d", b=B)
        o = out.rearrange("b (n p) d -> p n b d", p=BLK)
        for k in range(NBLK // YB):
            for b in range(B):
                sp.dma_start(yt[:, k * YB:(k + 1) * YB, b, :], y[:, k * YB:(k + 1) * YB, b, :]
                             ).then_inc(y_sems[k], 16)
        for k in range(NBLK // YB):
            sp.wait_ge(s["out_ready"], k + 1)
            for b in range(B):
                sp.dma_start(o[:, k * YB:(k + 1) * YB, b, :], acc[:, k * YB:(k + 1) * YB, b, :]
                             ).then_inc(s["out_stored"], 16)
        sp.wait_ge(s["out_stored"], 16 * B * (NBLK // YB))

    @block.gpsimd
    def _(pool):
        nc.gpsimd.memset(id2[:, :], 0.0).then_inc(s["id_ready"], 1)
        pool.wait_ge(s["id_ready"], 1)
        nc.gpsimd.affine_select(out=id2[:, :], in_=id2[:, :], compare_op=ALU.not_equal,
                                fill=1.0, base=0, pattern=[[-1, 64]], channel_multiplier=1
                                ).then_inc(s["id_ready"], 1)
        nc.gpsimd.iota(spare[:, :], pattern=[[1, CAP]], base=0, channel_multiplier=0,
                       allow_small_or_imprecise_dtypes=True).then_inc(s["spare_ready"], 1)
        pool.wait_ge(s["idx_ready"], 1)

        def indices(i):
            return (idx[:, i * EB:(i + 1) * EB] if isinstance(i, int)
                    else idx[:, bass.ds(i * EB, EB)])

        def gather(par, k):
            pool.indirect_dma_start(
                out=rows[:, par, k, :], out_offset=None, in_=scratch["rows"],
                in_offset=bass.IndirectOffsetOnAxis(ap=ic[:, par, k:k + 1], axis=0),
                bounds_check=N + CAP - 1).then_inc(gathered[par], 16)

        def scatter(i, par, ahead):
            pool.wait_ge(s["ys_ready"], i + 1)
            stand_alone(pool, s["pool_noted"])
            nc.gpsimd.tensor_copy(oc[:, par, :], indices(i)).then_inc(s["out_copied"], 1)
            pool.wait_ge(s["out_copied"], i + 1)
            stand_alone(pool, s["pool_noted"])
            if ahead:
                nc.gpsimd.tensor_copy(ic[:, par, :], indices(i + 2)).then_inc(s["idx_copied"], 1)
                pool.wait_ge(s["idx_copied"], i + 3)
                stand_alone(pool, s["pool_noted"])
            for k in range(EB):
                if not (isinstance(i, int) and i == 0 and k == 0):
                    pool.wait_ge(s["added"], 16 * (EB * i + k))
                    stand_alone(pool, s["pool_noted"])
                pool.indirect_dma_start(
                    out=scratch["y"],
                    out_offset=bass.IndirectOffsetOnAxis(ap=oc[:, par, k:k + 1], axis=0),
                    in_=ys[:, par, k, :], in_offset=None, bounds_check=N + CAP - 1,
                    compute_op=ALU.add).then_inc(s["added"], 16)
                if ahead:
                    gather(par, k)

        for i in range(2):
            nc.gpsimd.tensor_copy(ic[:, i, :], indices(i)).then_inc(s["idx_copied"], 1)
            pool.wait_ge(s["idx_copied"], i + 1)
            for k in range(EB):
                gather(i, k)
        scatter(0, 0, True)
        scatter(1, 1, True)
        with pool.Fori(1, NB // 2 - 1) as pair:
            for par in range(2):
                scatter(2 * pair + par, par, True)
        for i in range(NB - 2, NB):
            scatter(i, i % 2, False)
        pool.wait_ge(s["added"], 16 * E)

    @block.scalar
    def _(act):
        for t, n in ((sg, "shared_gate"), (su, "shared_up"), (sd, "shared_down")):
            act.dma_start(t[:, :, :], io[n].rearrange("(c p) f -> p c f", p=128)
                          ).then_inc(s["shared_arrived"], 16)

        def shared_silu(g, fc):
            act.wait_ge(s["g_mm"], FC * g + fc + 1)
            if not (isinstance(g, int) and g == 0):
                act.wait_ge(s["sh_ready"], FC * (g - 1) + fc + 1)
            nc.scalar.activation(sil[:, fc, :], bank_g[fc][:, :], ACT.Silu
                                 ).then_inc(s["sil_ready"], 1)

        for g in range(AHEAD):
            for fc in range(FC):
                shared_silu(g, fc)

        def batch(i, par, group):
            act.wait_ge(s["t_mm"], i + 1)
            nc.scalar.activation(rt[:, :, :, :], bank_t[:, :], ACT.Copy).then_inc(s["rt_ready"], 1)
            if group is not None:
                shared_silu(group, 0)
            act.wait_ge(s["h_mm"], i + 1)
            for half in range(2):
                h = bank_h[half][0:CAP, :].rearrange("p (k w f) -> p k w f", k=2, w=2)
                ins = nc.scalar.activation(hs[:, 2 * half:2 * half + 2, :], h[:, :, 0, :], ACT.Silu)
            ins.then_inc(s["silu_ready"], 1)
            if group is not None:
                shared_silu(group, 1)

        batches(act, batch)

    @block.vector
    def _(dve):
        def shared_mul(g, fc):
            dve.wait_ge(s["sil_ready"], FC * g + fc + 1)
            dve.wait_ge(s["u_mm"], FC * g + fc + 1)
            if not (isinstance(g, int) and g == 0):
                dve.wait_ge(s["d_mm"], TG * g)
            nc.vector.tensor_tensor(sh[:, fc, :], sil[:, fc, :], bank_u[fc][:, :], ALU.mult
                                    ).then_inc(s["sh_ready"], 1)

        def shared_add(g):
            for k in range(TG):
                dve.wait_ge(s["d_mm"], TG * g + k + 1)
                a = (acc[:, TG * g + k, :, :].rearrange("p b d -> p (b d)") if isinstance(g, int)
                     else acc[:, bass.ds(TG * g + k, 1), :, :].rearrange("p n b d -> p (n b d)"))
                nc.vector.tensor_tensor(a, a, bank_d[:, :], ALU.add).then_inc(s["acc_ready"], 1)

        link = link_on(dve, s["top_step"], 0)

        def top8(out, values, r):
            link(nc.vector.max(out[:, 8 * r:8 * r + 8], values))
            link(nc.vector.match_replace(out=values, in_to_replace=out[:, 8 * r:8 * r + 8],
                                         in_values=values, imm_value=-1.0))

        def acc_loaded(k):
            dve.wait_ge(acc_arrived[k], 16)

        dve.wait_ge(s["vq_arrived"], 16 * QUARTERS)
        for r in range(ROUNDS):
            top8(cand, vq[:, :], r)
            if r == 3:
                shared_mul(0, 0)
            if r == 5:
                shared_mul(0, 1)
        acc_loaded(0)
        shared_add(0)
        dve.wait_ge(s["cm_arrived"], 16 * QUARTERS)
        for r in range(ROUNDS):
            top8(sel, cm[:, :, :].rearrange("p q c -> p (q c)"), r)
            if r == 0:
                shared_mul(1, 0)
            if r == 4:
                shared_mul(1, 1)
        dve.wait_ge(s["spare_ready"], 1)
        link(nc.vector.scalar_tensor_tensor(out=idxf[:, 0, :], in0=sel[:, :], scalar=0.0,
                                            in1=spare[:, :], op0=ALU.is_equal, op1=ALU.mult))
        link(nc.vector.scalar_tensor_tensor(out=idxf[:, 1, :], in0=sel[:, :], scalar=-1.0,
                                            in1=idxf[:, 0, :], op0=ALU.mult, op1=ALU.add))
        link(nc.vector.tensor_scalar_add(idxf[:, 2, :], idxf[:, 1, :], float(N)))
        dve.wait_ge(s["sel_mm"], 1)
        nc.vector.tensor_copy(idx[:, :], bank_t[0:CAP, 0:E]).then_inc(s["idx_ready"], 1)
        shared_add(1)
        for fc in range(FC):
            shared_mul(2, fc)
        acc_loaded(1)
        shared_add(2)
        for fc in range(FC):
            shared_mul(3, fc)
        shared_add(3)
        for k in range(2, NBLK // YB):
            acc_loaded(k)

        def batch(i, par, group):
            if isinstance(i, int):
                dve.wait_ge(gathered[par], 16 * EB * (i // 2 + 1))
            else:
                dve.wait_ge(gathered[par], 8 * EB * (i - par) + 16 * EB)
            for k in range(EB):
                e = i * EB + k
                col = (rows[:, par, k, D + e:D + e + 1] if isinstance(i, int)
                       else rows[:, par, k, bass.ds(D + e, 1)])
                ins = nc.vector.tensor_copy(wc[:, par, k:k + 1], col)
            ins.then_inc(s["wc_ready"], 1)
            if group is not None:
                shared_mul(group, 0)
            dve.wait_ge(s["silu_ready"], i + 1)
            for half in range(2):
                h = bank_h[half][0:CAP, :].rearrange("p (k w f) -> p k w f", k=2, w=2)
                ins = nc.vector.tensor_tensor(hh[:, 2 * half:2 * half + 2, :],
                                              hs[:, 2 * half:2 * half + 2, :], h[:, :, 1, :],
                                              ALU.mult)
            ins.then_inc(s["hh_ready"], 1)
            if group is not None:
                shared_mul(group, 1)
            dve.wait_ge(s["ht_mm"], i + 1)
            nc.vector.tensor_copy(ht[:, :, :], bank_t[:, 0:EB * CAP]).then_inc(s["ht_ready"], 1)
            if group is not None:
                shared_add(group)
            dve.wait_ge(s["y_mm"], i + 1)
            for k in range(EB):
                ins = nc.vector.tensor_scalar(
                    ys[:, par, k, :], bank_h[k // 2][0:CAP, (k % 2) * D:(k % 2 + 1) * D],
                    wc[:, par, k:k + 1], None, ALU.mult)
            ins.then_inc(s["ys_ready"], 1)

        batches(dve, batch)
        for k in range(NBLK // YB):
            dve.wait_ge(y_sems[k], 16 * B)
            a = acc[:, k * YB:(k + 1) * YB, :, :].rearrange("p n b d -> p (n b d)")
            y = xt[:, k * YB:(k + 1) * YB, :, :, :].rearrange("p n c b t -> p (n c b t)")
            nc.vector.tensor_tensor(a, a, y, ALU.add).then_inc(s["out_ready"], 1)

    @block.tensor
    def _(pe):
        mm = nc.tensor.matmul

        def shared_up(g, fc):
            x = (xt[:, TG * g:TG * g + TG] if isinstance(g, int) else xt[:, bass.ds(TG * g, TG)])
            if not (isinstance(g, int) and g == 0):
                pe.wait_ge(s["sh_ready"], FC * (g - 1) + fc + 1)
            for w, bank_w, done in ((sg, bank_g, "g_mm"), (su, bank_u, "u_mm")):
                for c in range(NC):
                    ins = mm(bank_w[fc][:, :], w[:, c, fc * 128:(fc + 1) * 128],
                             x[:, :, c, :, :].rearrange("p n b t -> p n (b t)"),
                             start=c == 0, stop=c == NC - 1)
                ins.then_inc(s[done], 1)

        def shared_down(g):
            pe.wait_ge(s["sh_ready"], FC * g + FC)
            for k in range(TG):
                if k or not (isinstance(g, int) and g == 0):
                    pe.wait_ge(s["acc_ready"], TG * g + k)
                for b in range(B):
                    for fc in range(FC):
                        col = (k * B + b) * BLK
                        ins = mm(bank_d[:, b * D:(b + 1) * D], sh[:, fc, col:col + BLK],
                                 sd[:, fc, :], start=fc == 0, stop=fc == FC - 1)
                ins.then_inc(s["d_mm"], 1)

        pe.wait_ge(s["shared_arrived"], 48)
        for g in range(AHEAD):
            if g % 2 == 0:
                pe.wait_ge(xt_arrived[g // 2], 16)
            for fc in range(FC):
                shared_up(g, fc)
            if g == 1:
                pe.wait_ge(s["id_ready"], 2)
                pe.wait_ge(s["top_step"], 4 * ROUNDS + 3)
                nc.tensor.transpose(bank_t[0:CAP, 0:E], idxf[:, 2, :], id2[0:E, 0:E]
                                    ).then_inc(s["sel_mm"], 1)
            shared_down(g)
        for k in range(AHEAD // 2, NBLK // YB):
            pe.wait_ge(xt_arrived[k], 16)
        pe.wait_ge(s["idx_ready"], 1)

        def batch(i, par, group):
            if isinstance(i, int):
                pe.wait_ge(gathered[par], 16 * EB * (i // 2 + 1))
                pe.wait_ge(we_arrived[par], 48 * (i // 2 + 1))
            else:
                pe.wait_ge(gathered[par], 8 * EB * (i - par) + 16 * EB)
                pe.wait_ge(we_arrived[par], 24 * (i - par) + 48)
            if isinstance(i, int) and i == 0:
                pass
            else:
                pe.wait_ge(s["ht_ready"], i)
            stand_alone(pe, s["pe_noted"])
            for k in range(EB):
                for c in range(NC):
                    ins = nc.tensor.transpose(
                        bank_t[:, (k * NC + c) * CAP:(k * NC + c + 1) * CAP],
                        rows[:, par, k, c * 128:(c + 1) * 128], id2[:, :])
            ins.then_inc(s["t_mm"], 1)
            if group is not None:
                shared_up(group, 0)
            pe.wait_ge(s["rt_ready"], i + 1)
            if not (isinstance(i, int) and i == 0):
                pe.wait_ge(s["ys_ready"], i)
            for k in range(EB):
                for c in range(NC):
                    e = i * EB + k
                    w = (w13[:, e:e + 1, c, :, :] if isinstance(i, int)
                         else w13[:, bass.ds(e, 1), c, :, :])
                    ins = mm(bank_h[k // 2][0:CAP, (k % 2) * 2 * F:(k % 2 + 1) * 2 * F],
                             rt[:, k, c, :], w.rearrange("p e w f -> p (e w f)"),
                             start=c == 0, stop=c == NC - 1)
            ins.then_inc(s["h_mm"], 1)
            if group is not None:
                shared_up(group, 1)
            pe.wait_ge(s["hh_ready"], i + 1)
            stand_alone(pe, s["pe_noted"])
            for k in range(EB):
                ins = nc.tensor.transpose(bank_t[:, k * CAP:(k + 1) * CAP], hh[:, k, :], id2[:, :])
            ins.then_inc(s["ht_mm"], 1)
            if group is not None:
                shared_down(group)
            pe.wait_ge(s["ht_ready"], i + 1)
            for k in range(EB):
                e = i * EB + k
                w = w2[:, e:e + 1, :] if isinstance(i, int) else w2[:, bass.ds(e, 1), :]
                ins = mm(bank_h[k // 2][0:CAP, (k % 2) * D:(k % 2 + 1) * D], ht[:, k, :],
                         w.rearrange("p e d -> p (e d)"), start=True, stop=True)
            ins.then_inc(s["y_mm"], 1)

        batches(pe, batch)


def build(nc, args, out):
    io = dict(zip(("x", "Wq", "Wk", "Wv", "Wo", "betas", "gate_w", "gate_bias", "w1", "w2", "w3",
                   "shared_gate", "shared_up", "shared_down"), args))
    scratch = {
        "x1": nc.dram_tensor("x1_rows", (NBLK, 128, B * D), fp32).ap(),
        "x1t": nc.dram_tensor("x1_normed_t", (NBLK, 128, NC * B * BLK), fp32).ap(),
        "rows": nc.dram_tensor("expert_rows", (N + CAP, ROW), fp32).ap(),
        "picks": nc.dram_tensor("picks", (E, N), fp32).ap(),
        "y": nc.dram_tensor("expert_sums", (N + CAP, D), fp32).ap(),
    }
    scratch["y_parts"] = scratch["y"].rearrange("n d -> (n d)").rearrange(
        "(a p m) -> a p m", a=NBLK, p=128)
    with ExitStack() as ctx:
        attention(nc, ctx, io, scratch)
    with ExitStack() as ctx:
        experts(nc, ctx, io, scratch, out)


_INS = ['L0_attn_x', 'L0_attn_Wq', 'L0_attn_Wk', 'L0_attn_Wv', 'L0_attn_Wo', 'L0_attn_betas',
        'L0_ffn_gate_w', 'L0_ffn_gate_bias', 'L0_ffn_w1', 'L0_ffn_w2', 'L0_ffn_w3',
        'L0_ffn_shared_gate', 'L0_ffn_shared_up', 'L0_ffn_shared_down']
_OUTS = [((2, 2048, 256), 'float32')]


def kernel(**inputs):
    import numpy as _np
    import concourse.bacc as _bacc
    from concourse import mybir as _mybir
    from concourse.bass_utils import run_bass_kernel_spmd as _run

    nc = _bacc.Bacc("TRN2", target_bir_lowering=False, num_devices=1)
    arrays, args = {}, []
    for name in _INS:
        a = _np.ascontiguousarray(inputs[name])
        arrays[f"in_{name}_dram"] = a
        args.append(nc.dram_tensor(f"in_{name}_dram", a.shape, _mybir.dt.from_np(a.dtype),
                                   kind="ExternalInput").ap())
    outs = []
    for i, (shape, dtype) in enumerate(_OUTS):
        dt = _mybir.dt.from_np(_np.dtype(dtype))
        outs.append(nc.dram_tensor(f"out_{i}_dram", shape, dt, kind="ExternalOutput").ap())
    build(nc, args, outs[0])
    r = _run(nc, [arrays], core_ids=[0])
    got = tuple(r.results[0][f"out_{i}_dram"] for i in range(len(_OUTS)))
    return got[0]
```
